# Optimizing a Trainium2 kernel written in Bass

```python
import numpy as np
import jax
import jax.numpy as jnp

def _softmax(x, axis=-1):
    return jax.nn.softmax(x, axis=axis)

def _gelu(x):
    return jax.nn.gelu(x, approximate=True)

def _silu(x):
    return jax.nn.silu(x)

def _sigmoid(x):
    return jax.nn.sigmoid(x)

def _layernorm(x, axis=-1, eps=1e-05):
    m = jnp.mean(x, axis=axis, keepdims=True)
    v = jnp.var(x, axis=axis, keepdims=True)
    return (x - m) / jnp.sqrt(v + eps)

def _scatter_add(tgt, idx, src, axis=0):
    return tgt.at[idx].add(src)

def _segment_sum(src, seg, n):
    return jax.ops.segment_sum(src, seg, n)
kernel_name = 'mk_cond_seq_d4_seqx_r4_7df1fe'

def setup_inputs(seed: int=0):
    np.random.seed(seed)
    _w = jnp.asarray

    def _rec_inputs():
        import jax
        import jax.numpy as jnp
        _rk = jax.random.key(seed)
        x = 0.5 + 0.2887 * jax.random.normal(jax.random.fold_in(_rk, 1), (4, 512, 512), jnp.float32)
        _lenS = 512 - jax.random.randint(jax.random.fold_in(_rk, 7), (4,), 0, max(1, 512 // 4) + 1, jnp.int32)
        _lenS2 = 512 - jax.random.randint(jax.random.fold_in(_rk, 8), (4,), 0, max(1, 512 // 4) + 1, jnp.int32)
        itok_B_17_1546 = jax.random.randint(jax.random.fold_in(_rk, 12), (4,), 17, 1547, jnp.int32)
        itok_B_1_2 = jax.random.randint(jax.random.fold_in(_rk, 13), (4,), 1, 3, jnp.int32)
        return (x, itok_B_17_1546, itok_B_1_2, _lenS)
    x, itok_B_17_1546, itok_B_1_2, _lenS = _rec_inputs()

    def _L0_cond_setup():
        import jax, jax.numpy as jnp
        import numpy as np
        B, T, V = (8, 128, 512)
        H = 4 * V
        key = jax.random.key(seed)
        ks = jax.random.split(key, 16)
        s = lambda n: 1.0 / np.sqrt(n)
        inp = {'x': jax.random.uniform(ks[0], (B, T, V), dtype=jnp.float32), 'lens': jax.random.randint(ks[1], (B,), 1, T, dtype=jnp.int64), 'target_codes': jax.random.randint(ks[2], (B,), 0, V, dtype=jnp.int64), 'Wq': jax.random.normal(ks[3], (V, V), jnp.float32) * s(V), 'Wk': jax.random.normal(ks[4], (V, V), jnp.float32) * s(V), 'Wv': jax.random.normal(ks[5], (V, V), jnp.float32) * s(V), 'Wp': jax.random.normal(ks[6], (V, V), jnp.float32) * s(V), 'bp': jnp.zeros((V,), jnp.float32), 'cW1': jax.random.normal(ks[7], (V, H), jnp.float32) * s(V), 'cb1': jnp.zeros((H,), jnp.float32), 'cW2': jax.random.normal(ks[8], (H, V), jnp.float32) * s(H), 'cb2': jnp.zeros((V,), jnp.float32), 'mW1': jax.random.normal(ks[9], (2 * V, H), jnp.float32) * s(2 * V), 'mb1': jnp.zeros((H,), jnp.float32), 'mW2': jax.random.normal(ks[10], (H, V), jnp.float32) * s(H), 'mb2': jnp.zeros((V,), jnp.float32)}
        return inp
    _L0_cond_all = _L0_cond_setup()
    _L0_cond_in = {k: v for k, v in _L0_cond_all.items() if k in ('Wq', 'Wk', 'Wv', 'Wp', 'bp', 'cW1', 'cb1', 'cW2', 'cb2', 'mW1', 'mb1', 'mW2', 'mb2')}
    del _L0_cond_all

    def _L1_cond_setup():
        import jax, jax.numpy as jnp
        import numpy as np
        H = 512
        K = 256
        R = 3
        B = 8
        S = 512
        LN_EPS = 1e-05
        key = jax.random.key(seed)
        ks = jax.random.split(key, 8)
        sd_d = 1.0 / np.sqrt(H)
        sd_u = 1.0 / np.sqrt(K)
        return {'role': jax.random.randint(ks[0], (B,), 0, R), 'hidden_states': jax.random.normal(ks[1], (B, S, H), dtype=jnp.float32), 'W_down': jax.random.uniform(ks[2], (R, H, K), jnp.float32, -sd_d, sd_d), 'b_down': jax.random.uniform(ks[3], (R, K), jnp.float32, -sd_d, sd_d), 'W_up': jax.random.uniform(ks[4], (R, K, H), jnp.float32, -sd_u, sd_u), 'b_up': jax.random.uniform(ks[5], (R, H), jnp.float32, -sd_u, sd_u), 'gamma': jnp.ones((R, H), jnp.float32), 'beta': jnp.zeros((R, H), jnp.float32)}
    _L1_cond_all = _L1_cond_setup()
    _L1_cond_in = {k: v for k, v in _L1_cond_all.items() if k in ('W_down', 'b_down', 'W_up', 'b_up', 'gamma', 'beta')}
    del _L1_cond_all

    def _L2_cond_setup():
        import jax, jax.numpy as jnp
        import numpy as np
        B, T, V = (8, 128, 512)
        H = 4 * V
        key = jax.random.key(seed)
        ks = jax.random.split(key, 16)
        s = lambda n: 1.0 / np.sqrt(n)
        inp = {'x': jax.random.uniform(ks[0], (B, T, V), dtype=jnp.float32), 'lens': jax.random.randint(ks[1], (B,), 1, T, dtype=jnp.int64), 'target_codes': jax.random.randint(ks[2], (B,), 0, V, dtype=jnp.int64), 'Wq': jax.random.normal(ks[3], (V, V), jnp.float32) * s(V), 'Wk': jax.random.normal(ks[4], (V, V), jnp.float32) * s(V), 'Wv': jax.random.normal(ks[5], (V, V), jnp.float32) * s(V), 'Wp': jax.random.normal(ks[6], (V, V), jnp.float32) * s(V), 'bp': jnp.zeros((V,), jnp.float32), 'cW1': jax.random.normal(ks[7], (V, H), jnp.float32) * s(V), 'cb1': jnp.zeros((H,), jnp.float32), 'cW2': jax.random.normal(ks[8], (H, V), jnp.float32) * s(H), 'cb2': jnp.zeros((V,), jnp.float32), 'mW1': jax.random.normal(ks[9], (2 * V, H), jnp.float32) * s(2 * V), 'mb1': jnp.zeros((H,), jnp.float32), 'mW2': jax.random.normal(ks[10], (H, V), jnp.float32) * s(H), 'mb2': jnp.zeros((V,), jnp.float32)}
        return inp
    _L2_cond_all = _L2_cond_setup()
    _L2_cond_in = {k: v for k, v in _L2_cond_all.items() if k in ('Wq', 'Wk', 'Wv', 'Wp', 'bp', 'cW1', 'cb1', 'cW2', 'cb2', 'mW1', 'mb1', 'mW2', 'mb2')}
    del _L2_cond_all

    def _L3_cond_setup():
        import jax, jax.numpy as jnp
        import numpy as np
        B, S, H = (8, 512, 512)
        BN = 256
        E = 3
        LN_EPS = 1e-05
        key = jax.random.key(seed)
        ks = jax.random.split(key, 8)
        stream = jax.random.randint(ks[0], (B,), 0, E, dtype=jnp.int32)
        hidden_states = jax.random.normal(ks[1], (B, S, H), dtype=jnp.float32)
        W_down = jax.random.normal(ks[2], (E, H, BN), dtype=jnp.float32) * 0.02
        b_down = jnp.zeros((E, BN), dtype=jnp.float32)
        W_up = jax.random.normal(ks[3], (E, BN, H), dtype=jnp.float32) * 0.02
        b_up = jnp.zeros((E, H), dtype=jnp.float32)
        ln_w = jnp.ones((E, H), dtype=jnp.float32)
        ln_b = jnp.zeros((E, H), dtype=jnp.float32)
        return {'stream': stream, 'hidden_states': hidden_states, 'W_down': W_down, 'b_down': b_down, 'W_up': W_up, 'b_up': b_up, 'ln_w': ln_w, 'ln_b': ln_b}
    _L3_cond_all = _L3_cond_setup()
    _L3_cond_in = {k: v for k, v in _L3_cond_all.items() if k in ('W_down', 'b_down', 'W_up', 'b_up', 'ln_w', 'ln_b')}
    del _L3_cond_all
    return {'x': x, 'itok_B_17_1546': itok_B_17_1546, 'itok_B_1_2': itok_B_1_2, '_lenS': _lenS, 'L0_cond_Wq': _L0_cond_in['Wq'], 'L0_cond_Wk': _L0_cond_in['Wk'], 'L0_cond_Wv': _L0_cond_in['Wv'], 'L0_cond_Wp': _L0_cond_in['Wp'], 'L0_cond_bp': _L0_cond_in['bp'], 'L0_cond_cW1': _L0_cond_in['cW1'], 'L0_cond_cb1': _L0_cond_in['cb1'], 'L0_cond_cW2': _L0_cond_in['cW2'], 'L0_cond_cb2': _L0_cond_in['cb2'], 'L0_cond_mW1': _L0_cond_in['mW1'], 'L0_cond_mb1': _L0_cond_in['mb1'], 'L0_cond_mW2': _L0_cond_in['mW2'], 'L0_cond_mb2': _L0_cond_in['mb2'], 'L1_cond_W_down': _L1_cond_in['W_down'], 'L1_cond_b_down': _L1_cond_in['b_down'], 'L1_cond_W_up': _L1_cond_in['W_up'], 'L1_cond_b_up': _L1_cond_in['b_up'], 'L1_cond_gamma': _L1_cond_in['gamma'], 'L1_cond_beta': _L1_cond_in['beta'], 'L2_cond_Wq': _L2_cond_in['Wq'], 'L2_cond_Wk': _L2_cond_in['Wk'], 'L2_cond_Wv': _L2_cond_in['Wv'], 'L2_cond_Wp': _L2_cond_in['Wp'], 'L2_cond_bp': _L2_cond_in['bp'], 'L2_cond_cW1': _L2_cond_in['cW1'], 'L2_cond_cb1': _L2_cond_in['cb1'], 'L2_cond_cW2': _L2_cond_in['cW2'], 'L2_cond_cb2': _L2_cond_in['cb2'], 'L2_cond_mW1': _L2_cond_in['mW1'], 'L2_cond_mb1': _L2_cond_in['mb1'], 'L2_cond_mW2': _L2_cond_in['mW2'], 'L2_cond_mb2': _L2_cond_in['mb2'], 'L3_cond_W_down': _L3_cond_in['W_down'], 'L3_cond_b_down': _L3_cond_in['b_down'], 'L3_cond_W_up': _L3_cond_in['W_up'], 'L3_cond_b_up': _L3_cond_in['b_up'], 'L3_cond_ln_w': _L3_cond_in['ln_w'], 'L3_cond_ln_b': _L3_cond_in['ln_b']}

def reference(x, itok_B_17_1546, itok_B_1_2, _lenS, L0_cond_Wq, L0_cond_Wk, L0_cond_Wv, L0_cond_Wp, L0_cond_bp, L0_cond_cW1, L0_cond_cb1, L0_cond_cW2, L0_cond_cb2, L0_cond_mW1, L0_cond_mb1, L0_cond_mW2, L0_cond_mb2, L1_cond_W_down, L1_cond_b_down, L1_cond_W_up, L1_cond_b_up, L1_cond_gamma, L1_cond_beta, L2_cond_Wq, L2_cond_Wk, L2_cond_Wv, L2_cond_Wp, L2_cond_bp, L2_cond_cW1, L2_cond_cb1, L2_cond_cW2, L2_cond_cb2, L2_cond_mW1, L2_cond_mb1, L2_cond_mW2, L2_cond_mb2, L3_cond_W_down, L3_cond_b_down, L3_cond_W_up, L3_cond_b_up, L3_cond_ln_w, L3_cond_ln_b):
    import jax
    import jax.numpy as jnp

    def _L0_cond_ref(x, lens, target_codes, Wq, Wk, Wv, Wp, bp, cW1, cb1, cW2, cb2, mW1, mb1, mW2, mb2):
        import jax, jax.numpy as jnp
        import numpy as np
        B, T, V = (8, 128, 512)
        H = 4 * V
        scale = V ** (-0.5)
        q = x @ Wq
        k = x @ Wk
        v = x @ Wv
        attn = jnp.einsum('btd,bTd->btT', q, k) * scale
        attn = jax.nn.softmax(attn, axis=-1)
        attn_out = jnp.einsum('btT,bTd->btd', attn, v) @ Wp + bp
        target_embed = jax.nn.one_hot(target_codes, V, dtype=x.dtype)[:, None, :]
        cms_out = jax.nn.gelu(attn_out @ cW1 + cb1, approximate=False) @ cW2 + cb2
        cms_out = cms_out + target_embed
        concat = jnp.concatenate([attn_out, cms_out], axis=-1)
        modifier = jax.nn.gelu(concat @ mW1 + mb1, approximate=False) @ mW2 + mb2
        out = jnp.clip(x + cms_out + modifier, 0.0, 1.0)
        return out

    def _L1_cond_ref(role, hidden_states, W_down, b_down, W_up, b_up, gamma, beta):
        import jax, jax.numpy as jnp
        import numpy as np
        H = 512
        K = 256
        R = 3
        B = 8
        S = 512
        LN_EPS = 1e-05
        h = jnp.einsum('bsh,bhk->bsk', hidden_states, W_down[role]) + b_down[role][:, None, :]
        h = jax.nn.gelu(h, approximate=False)
        u = jnp.einsum('bsk,bkh->bsh', h, W_up[role]) + b_up[role][:, None, :]
        y = hidden_states + u
        mean = jnp.mean(y, axis=-1, keepdims=True)
        var = jnp.mean(jnp.square(y - mean), axis=-1, keepdims=True)
        yn = (y - mean) * jax.lax.rsqrt(var + LN_EPS)
        return yn * gamma[role][:, None, :] + beta[role][:, None, :]

    def _L2_cond_ref(x, lens, target_codes, Wq, Wk, Wv, Wp, bp, cW1, cb1, cW2, cb2, mW1, mb1, mW2, mb2):
        import jax, jax.numpy as jnp
        import numpy as np
        B, T, V = (8, 128, 512)
        H = 4 * V
        scale = V ** (-0.5)
        q = x @ Wq
        k = x @ Wk
        v = x @ Wv
        attn = jnp.einsum('btd,bTd->btT', q, k) * scale
        attn = jax.nn.softmax(attn, axis=-1)
        attn_out = jnp.einsum('btT,bTd->btd', attn, v) @ Wp + bp
        target_embed = jax.nn.one_hot(target_codes, V, dtype=x.dtype)[:, None, :]
        cms_out = jax.nn.gelu(attn_out @ cW1 + cb1, approximate=False) @ cW2 + cb2
        cms_out = cms_out + target_embed
        concat = jnp.concatenate([attn_out, cms_out], axis=-1)
        modifier = jax.nn.gelu(concat @ mW1 + mb1, approximate=False) @ mW2 + mb2
        out = jnp.clip(x + cms_out + modifier, 0.0, 1.0)
        return out

    def _L3_cond_ref(stream, hidden_states, W_down, b_down, W_up, b_up, ln_w, ln_b):
        import jax, jax.numpy as jnp
        import numpy as np
        B, S, H = (8, 512, 512)
        BN = 256
        E = 3
        LN_EPS = 1e-05
        Wd = W_down[stream]
        bd = b_down[stream]
        Wu = W_up[stream]
        bu = b_up[stream]
        g = ln_w[stream]
        b = ln_b[stream]
        residual = hidden_states
        h = jnp.einsum('bsh,bhk->bsk', hidden_states, Wd) + bd[:, None, :]
        h = jax.nn.gelu(h, approximate=False)
        h = jnp.einsum('bsk,bkh->bsh', h, Wu) + bu[:, None, :]
        h = residual + h
        mean = jnp.mean(h, axis=-1, keepdims=True)
        var = jnp.mean(jnp.square(h - mean), axis=-1, keepdims=True)
        h = (h - mean) * jax.lax.rsqrt(var + LN_EPS)
        return h * g[:, None, :] + b[:, None, :]
    x = _L0_cond_ref(x, _lenS, itok_B_17_1546, L0_cond_Wq, L0_cond_Wk, L0_cond_Wv, L0_cond_Wp, L0_cond_bp, L0_cond_cW1, L0_cond_cb1, L0_cond_cW2, L0_cond_cb2, L0_cond_mW1, L0_cond_mb1, L0_cond_mW2, L0_cond_mb2)
    x = _L1_cond_ref(itok_B_1_2, x, L1_cond_W_down, L1_cond_b_down, L1_cond_W_up, L1_cond_b_up, L1_cond_gamma, L1_cond_beta)
    x = _L2_cond_ref(x, _lenS, itok_B_17_1546, L2_cond_Wq, L2_cond_Wk, L2_cond_Wv, L2_cond_Wp, L2_cond_bp, L2_cond_cW1, L2_cond_cb1, L2_cond_cW2, L2_cond_cb2, L2_cond_mW1, L2_cond_mb1, L2_cond_mW2, L2_cond_mb2)
    x = _L3_cond_ref(itok_B_1_2, x, L3_cond_W_down, L3_cond_b_down, L3_cond_W_up, L3_cond_b_up, L3_cond_ln_w, L3_cond_ln_b)
    return x

_drawn_inputs = setup_inputs


def setup_inputs(seed=0):
    import zlib

    import numpy as np

    out = dict(_drawn_inputs(seed))
    spreads = {'L0_cond_bp': (0.0, 0.1),
     'L0_cond_cb1': (0.0, 0.1),
     'L0_cond_cb2': (0.0, 0.1),
     'L0_cond_mb1': (0.0, 0.1),
     'L0_cond_mb2': (0.0, 0.1),
     'L1_cond_gamma': (1.0, 0.2),
     'L1_cond_beta': (0.0, 0.1),
     'L2_cond_bp': (0.0, 0.1),
     'L2_cond_cb1': (0.0, 0.1),
     'L2_cond_cb2': (0.0, 0.1),
     'L2_cond_mb1': (0.0, 0.1),
     'L2_cond_mb2': (0.0, 0.1),
     'L3_cond_b_down': (0.0, 0.1),
     'L3_cond_b_up': (0.0, 0.1),
     'L3_cond_ln_w': (1.0, 0.2),
     'L3_cond_ln_b': (0.0, 0.1)}
    factors = {'L0_cond_Wq': 8.0, 'L0_cond_Wk': 7.988}
    for name, (base, spread) in spreads.items():
        noise = np.random.default_rng([zlib.crc32(name.encode()), seed]).standard_normal(out[name].shape)
        drawn = base * np.exp(spread * noise) if base else spread * noise
        out[name] = jnp.asarray(drawn.astype(out[name].dtype))
    for name, factor in factors.items():
        out[name] = (out[name] * factor).astype(out[name].dtype)
    return out
```

```python
from contextlib import ExitStack

import numpy as np
import concourse.bass as bass
from concourse import mybir

F32, F32R, I32 = mybir.dt.float32, mybir.dt.float32r, mybir.dt.int32
ACT, ALU, AX = mybir.ActivationFunctionType, mybir.AluOpType, mybir.AxisListType

P = 128
D = 512
T = 512
KT = D // P
HID = 2048
HC = 256
MC = HC // P
CH = HID // HC
BATCHES, GROUP, LAYERS, ROLES = 4, 2, 2, 3
ROUNDS = LAYERS * BATCHES // GROUP
EPS = 1e-5
SCALE = float(D) ** -0.5
PIECE = 1024

BP, CB1, CB2, MB1, MB2 = 0, KT, KT + HID // P, 2 * KT + HID // P, 2 * KT + 2 * HID // P
NVEC = 3 * KT + 2 * HID // P
BD, BU, GA, BE = 0, MC, MC + KT, MC + 2 * KT
NAVEC = MC + 3 * KT

CMS_PIECES, MOD_PIECES = 2, 3
PC_A, PC_U = 0, 2
PC_CMS = 4
PC_MOD = PC_CMS + CMS_PIECES * CH
PC_ADA = PC_MOD + MOD_PIECES * CH
PC_ROUND = PC_ADA + 2 * GROUP
FOLDS = 2 * LAYERS
PC_FOLD = 4 * FOLDS

M_Y0, M_V0, M_S0, M_Y1, M_V1, M_T0, M_S1, M_O0, M_T1, M_O1 = range(0, 40, KT)
M_CMS = 40
M_CHUNK = GROUP * (MC + KT)
M_MOD = M_CMS + M_CHUNK * CH
M_DOWN = M_MOD + M_CHUNK * CH
M_UP = M_DOWN + GROUP * MC
M_ROUND = M_UP + GROUP * KT
M_FOLD = FOLDS * KT

S_Y0, S_V0, S_Y1, S_V1, S_P0, S_O0, S_P1, S_O1 = range(0, 32, KT)
S_CH = 32
S_CMS = S_CH + GROUP * MC * CH
S_MH = S_CMS + GROUP * KT
S_Z = S_MH + GROUP * MC * CH
S_AH = S_Z + GROUP * KT
S_ROUND = S_AH + GROUP * MC

C_CMS = GROUP * KT
C_MOD = C_CMS + GROUP * KT * CH
C_UP = C_MOD + GROUP * KT * CH
C_ROUND = C_UP + GROUP * KT

V0_BANKS = (6, 7, 4, 5)


def build(nc, x_t, codes, roles, fold_w, cms_w, mod_w, ada_w, vecs, avecs, out):
    folded = nc.dram_tensor("folded", (FOLDS, 2, P, PIECE), F32, kind="Internal").ap()
    ctx = ExitStack()
    with ctx:
        def sb(name, shape, dt=F32):
            return ctx.enter_context(nc.sbuf_tensor(name, shape, dt))

        def sem(name):
            return ctx.enter_context(nc.semaphore(name))

        xs = sb("xs", [P, 2, GROUP, KT, T])
        xa_hi, xa_lo = (sb(f"xa_{n}", [P, GROUP, KT, T], F32R) for n in ("hi", "lo"))
        vc_hi, vc_lo = (sb(f"vc_{n}", [P, GROUP, KT, T], F32R) for n in ("hi", "lo"))
        yp_hi, yp_lo = (sb(f"yp_{n}", [P, KT, T], F32R) for n in ("hi", "lo"))
        ph_hi, ph_lo = (sb(f"ph_{n}", [P, KT, T], F32R) for n in ("hi", "lo"))
        pc = sb("pc", [P, GROUP, KT, T])
        ring = sb("ring", [P, 2, 2, 3, PIECE], F32R)
        staging = sb("staging", [P, 2, PIECE])
        graw = sb("graw", [P, 2, T])
        lsum = sb("lsum", [P, GROUP, T])
        ls_hi, ls_lo = (sb(f"ls_{n}", [P, GROUP, T], F32R) for n in ("hi", "lo"))
        ident = sb("ident", [P, P])
        mean_w = sb("mean_w", [P, P], F32R)
        ones = sb("ones", [P, P])
        vec = sb("vec", [P, LAYERS, NVEC])
        avec = sb("avec", [P, LAYERS * BATCHES, NAVEC])
        cbias = sb("cbias", [P, LAYERS * BATCHES, KT])
        code_i = sb("code_i", [P, BATCHES], I32)
        code_f = sb("code_f", [P, BATCHES])
        role_sb = sb("role_sb", [1, BATCHES], I32)
        feat_i = sb("feat_i", [P, KT], I32)
        feat_f = sb("feat_f", [P, KT])
        hot = sb("hot", [P, BATCHES, KT])
        eps = sb("eps", [P, 1])
        smax = sb("smax", [P, GROUP * KT])
        nmax = sb("nmax", [P, GROUP * KT])
        rsum = sb("rsum", [P, GROUP * KT])
        rinv = sb("rinv", [P, GROUP * KT])
        bank = [ctx.enter_context(nc.psum_tensor(f"bank{i}", [P, 512], F32)) for i in range(8)]

        stage_in = [sem("stage_in0"), sem("stage_in1")]
        w_hi, w_lo = sem("w_hi"), sem("w_lo")
        mm_done = sem("mm_done")
        hi_ready, lo_ready = sem("hi_ready"), sem("lo_ready")
        x_hi, x_lo = sem("x_hi"), sem("x_lo")
        fold_raw = sem("fold_raw")
        fold_out = [sem("fold_out0"), sem("fold_out1")]
        x_in = [sem("x_in0"), sem("x_in1")]
        small_in, role_in, avec_in = sem("small_in"), sem("role_in"), sem("avec_in")
        const_ready, iota_ready, code_ready, hot_ready, cbias_ready = (
            sem(n) for n in ("const_ready", "iota_ready", "code_ready", "hot_ready", "cbias_ready"))
        smax_done, nmax_ready, exp_done, rinv_done, p_ready = (
            sem(n) for n in ("smax_done", "nmax_ready", "exp_done", "rinv_done", "p_ready"))
        raw_ready, acc_added, res_added, z_low, z_ready = (
            sem(n) for n in ("raw_ready", "acc_added", "res_added", "z_low", "z_ready"))
        sum_step, ls_hi_ready, ls_lo_ready, stat_done, centred, squared, std_ready, rstd_ready, scaled, x_final = (
            sem(n) for n in ("sum_step", "ls_hi_ready", "ls_lo_ready", "stat_done", "centred", "squared",
                             "std_ready", "rstd_ready", "scaled", "x_final"))
        out_done = sem("out_done")
        sp_passed, act_passed, dve_passed = sem("sp_passed"), sem("act_passed"), sem("dve_passed")

        def fold_places(f):
            if f % 2 == 0:
                return (vc_hi[:, 0], vc_lo[:, 0]), (vc_hi[:, 1], vc_lo[:, 1])
            return (yp_hi[:, :, :], yp_lo[:, :, :]), (ph_hi[:, :, :], ph_lo[:, :, :])

        def fold_piece(f, q):
            part = fold_places(f)[q // 2]
            return [x[:, 2 * (q % 2):2 * (q % 2) + 2, :].rearrange("p k n -> p (k n)") for x in part]

        def stage(q):
            return staging[:, q % 2, :]

        def f32(ap):
            return ap.bitcast(F32)

        def xs_tile(g, b, k):
            return xs[:, bass.ds(g, 1), b, k, :].rearrange("p a n -> p (a n)") if not isinstance(g, int) else xs[:, g, b, k, :]

        def col(t, row, c):
            return t[:, bass.ds(row, 1), c] if not isinstance(row, int) else t[:, row, c:c + 1]

        def column(t, row, c):
            width = t.shape[2]
            flat = t[:, :, :].rearrange("p r c -> p (r c)")
            at = row * width + c
            return flat[:, at:at + 1] if isinstance(at, int) else flat[:, bass.ds(at, 1)]

        block = ctx.enter_context(nc.Block())

        @block.sync
        def _(sp):
            def load(src, free_at, k):
                sp.wait_ge(w_lo, free_at)
                sp.dma_start(stage(k), src).then_inc(stage_in[k % 2], 16)

            for q in range(PC_FOLD):
                if q >= 2:
                    load(fold_w[q], q - 1, q)
                else:
                    sp.dma_start(stage(q), fold_w[q]).then_inc(stage_in[q], 16)

            with sp.Fori(0, ROUNDS) as r:
                base = r * PC_ROUND + PC_FOLD
                layer = r // 2
                for w in range(2):
                    sp.wait_ge(fold_out[w], layer * 16 + 16)
                    sp.sem_inc(sp_passed, 1)
                    for q in range(2):
                        src = folded[bass.ds(layer * 2 + w, 1), q, :, :].rearrange("a p n -> (a p) n")
                        load(src, base + (2 * w + q - 1), q)
                with sp.Fori(0, CH) as c:
                    for q in range(CMS_PIECES):
                        src = cms_w[bass.ds(layer * (CMS_PIECES * CH) + c * CMS_PIECES + q, 1), :, :].rearrange("a p n -> (a p) n")
                        load(src, base + c * CMS_PIECES + (PC_CMS + q - 1), q)
                with sp.Fori(0, CH // 2) as c2:
                    for q in range(2 * MOD_PIECES):
                        src = mod_w[bass.ds(layer * (MOD_PIECES * CH) + c2 * (2 * MOD_PIECES) + q, 1), :, :].rearrange("a p n -> (a p) n")
                        load(src, base + c2 * (2 * MOD_PIECES) + (PC_MOD + q - 1), q)
                sp.wait_ge(role_in, 16)
                for b in range(GROUP):
                    role = sp.value_load(role_sb[0:1, bass.ds((r % 2) * GROUP + b, 1)], min_val=0, max_val=ROLES - 1)
                    for q in range(2):
                        src = ada_w[bass.ds((layer * ROLES + role) * 2 + q, 1), :, :].rearrange("a p n -> (a p) n")
                        load(src, base + (PC_ADA + 2 * b + q - 1), q)
            for n in range(2):
                sp.wait_ge(fold_out[n], 16 * LAYERS)

        @block.gpsimd
        def _(pool):
            pool.memset(ident[:, :], 0.0).then_inc(iota_ready, 1)
            pool.memset(ones[:, :], 1.0)
            pool.memset(eps[:, :], EPS)
            pool.iota(feat_i[:, :], pattern=[[P, KT]], base=0, channel_multiplier=1).then_inc(iota_ready, 1)
            pool.wait_ge(iota_ready, 1)
            pool.affine_select(out=ident[:, :], in_=ident[:, :], compare_op=ALU.not_equal, fill=1.0,
                               base=0, pattern=[[-1, P]], channel_multiplier=1).then_inc(const_ready, 1)

        @block.tensor
        def _(pe):
            def tile(dst, parts):
                last = len(parts) - 1
                for n, (lh, ll, rh, rl) in enumerate(parts):
                    pe.matmul(dst, lh, rh, start=n == 0, stop=False)
                    pe.matmul(dst, lh, rl, start=False, stop=False)
                    done = pe.matmul(dst, ll, rh, start=False, stop=n == last)
                return done.then_inc(mm_done, 1)

            def slot_w(slot, piece, lo, hi):
                return ring[:, slot, 0, piece, lo:hi], ring[:, slot, 1, piece, lo:hi]

            def fold(f):
                pe.wait_ge(w_lo, 4 * f + 4)
                (lh, ll), (rh, rl) = fold_places(f)
                for m in range(KT):
                    if f >= 2:
                        pe.wait_ge(fold_raw, 4 * (f - 2) + m + 1)
                    tile(bank[4 * (f % 2) + m][:, :],
                         [(lh[:, k, m * P:(m + 1) * P], ll[:, k, m * P:(m + 1) * P], rh[:, k, :], rl[:, k, :])
                          for k in range(KT)])

            def project_y(b, m, dst):
                tile(dst, [(*slot_w(0, k // 2, (k % 2) * D + m * P, (k % 2) * D + (m + 1) * P),
                            xa_hi[:, b, k, :], xa_lo[:, b, k, :]) for k in range(KT)])

            def project_v(b, m, dst):
                tile(dst, [(xa_hi[:, b, k, m * P:(m + 1) * P], xa_lo[:, b, k, m * P:(m + 1) * P],
                            *slot_w(1, k // 2, (k % 2) * D, (k % 2 + 1) * D)) for k in range(KT)])

            def scores(b, m, dst):
                tile(dst, [(yp_hi[:, k, m * P:(m + 1) * P], yp_lo[:, k, m * P:(m + 1) * P],
                            xa_hi[:, b, k, :], xa_lo[:, b, k, :]) for k in range(KT)])

            def transposed(b, j, dst):
                for i in range(KT):
                    done = pe.transpose(dst[:, i * P:(i + 1) * P], pc[:, b, i, j * P:(j + 1) * P], ident[:, :])
                done.then_inc(mm_done, 1)

            def attended(b, m, dst, p_hi, p_lo):
                tile(dst, [(vc_hi[:, b, k, m * P:(m + 1) * P], vc_lo[:, b, k, m * P:(m + 1) * P],
                            p_hi[:, k, :], p_lo[:, k, :]) for k in range(KT)])

            def stat(dst, b):
                pe.matmul(dst, mean_w[:, :], ls_hi[:, b, :], start=True, stop=False)
                pe.matmul(dst, mean_w[:, :], ls_lo[:, b, :], start=False, stop=True).then_inc(stat_done, 1)

            def norm_stat(r, what, banks):
                for b in range(GROUP):
                    pe.wait_ge(ls_lo_ready, r * 4 + (2 * what + b + 1))
                    stat(bank[banks[b]][:, :], b)

            def attend(r, before):
                w0, s0, e0 = r * PC_ROUND + PC_FOLD, r * S_ROUND, r * (GROUP * KT)
                pe.wait_ge(w_lo, w0 + (PC_A + 2))
                pe.wait_ge(x_lo, e0 + KT)
                for m in range(KT):
                    if before is None:
                        pe.wait_ge(fold_raw, 8 + m + 1)
                    else:
                        pe.wait_ge(acc_added, before * C_ROUND + (C_UP + KT + m + 1))
                    project_y(0, m, bank[m][:, :])
                if before is not None:
                    norm_stat(before, 0, (4, 5))
                pe.wait_ge(w_lo, w0 + (PC_U + 2))
                for m in range(KT):
                    if before is None:
                        pe.wait_ge(fold_raw, 12 + KT)
                    elif m >= 2:
                        pe.wait_ge(centred, before * (GROUP * KT) + (m - 1) * KT)
                    project_v(0, m, bank[V0_BANKS[m]][:, :])
                pe.wait_ge(lo_ready, s0 + (S_Y0 + KT))
                for m in range(KT):
                    scores(0, m, bank[m][:, :])
                if before is not None:
                    pe.wait_ge(lo_ready, s0 + (S_V0 + 2))
                    norm_stat(before, 1, (6, 7))
                pe.wait_ge(x_lo, e0 + 2 * KT)
                pe.wait_ge(lo_ready, s0 + (S_V0 + KT))
                for m in range(KT):
                    if before is not None and m >= 2:
                        pe.wait_ge(std_ready, before * GROUP + (m - 1))
                    project_y(1, m, bank[4 + m][:, :])
                for m in range(KT):
                    pe.wait_ge(exp_done, e0 + (m + 1))
                    project_v(1, m, bank[m][:, :])
                pe.wait_ge(p_ready, e0 + KT)
                for m in range(KT):
                    pe.wait_ge(lo_ready, s0 + (S_Y1 + m + 1))
                    transposed(0, m, bank[4 + m])
                for m in range(KT):
                    pe.wait_ge(lo_ready, s0 + (S_V1 + m + 1))
                    scores(1, m, bank[m][:, :])
                pe.wait_ge(lo_ready, s0 + (S_P0 + KT))
                for m in range(KT):
                    attended(0, m, bank[4 + m][:, :], ph_hi, ph_lo)
                pe.wait_ge(p_ready, e0 + 2 * KT)
                for m in range(KT):
                    transposed(1, m, bank[m])
                pe.wait_ge(lo_ready, s0 + (S_P1 + KT))
                for m in range(KT):
                    attended(1, m, bank[4 + m][:, :], yp_hi, yp_lo)

            def chunk(slot, w_at, h_at, c_at, pieces, inputs, inputs_at):
                up = pieces - 1
                per = KT if up == 1 else 4
                pe.wait_ge(w_lo, w_at + up)
                for b in range(GROUP):
                    pe.wait_ge(lo_ready, inputs_at[b])
                    for m in range(MC):
                        pe.wait_ge(hi_ready, h_at + (MC * b + m - 3))
                        tile(bank[MC * b + m][:, :],
                             [(*slot_w(slot, k // per, (k % per) * HC + m * P, (k % per) * HC + (m + 1) * P),
                               *(x[:, b, kk, :] for x in pair))
                              for k, (pair, kk) in enumerate(inputs)])
                pe.wait_ge(w_lo, w_at + pieces)
                for b in range(GROUP):
                    pe.wait_ge(lo_ready, h_at + (MC * b + MC))
                    for m in range(KT):
                        pe.wait_ge(acc_added, c_at + (KT * b + m - 3))
                        tile(bank[4 + m][:, :],
                             [(*slot_w(slot, up, k * D + m * P, k * D + (m + 1) * P),
                               ph_hi[:, MC * b + k, :], ph_lo[:, MC * b + k, :]) for k in range(MC)])

            attn_in = [((xa_hi, xa_lo), k) for k in range(KT)]
            cms_in = [((vc_hi, vc_lo), k) for k in range(KT)]

            def mlp(r):
                w0, s0, c0 = r * PC_ROUND + PC_FOLD, r * S_ROUND, r * C_ROUND
                with pe.Fori(0, CH // 2) as c2:
                    for u in range(2):
                        chunk(u, w0 + c2 * (2 * CMS_PIECES) + (PC_CMS + CMS_PIECES * u),
                              s0 + c2 * (2 * GROUP * MC) + (S_CH + GROUP * MC * u),
                              c0 + c2 * (2 * GROUP * KT) + (C_CMS + GROUP * KT * u),
                              CMS_PIECES, attn_in, [s0 + (S_O0 + KT), s0 + (S_O1 + KT)])
                with pe.Fori(0, CH // 2) as c2:
                    for u in range(2):
                        chunk(u, w0 + c2 * (2 * MOD_PIECES) + (PC_MOD + MOD_PIECES * u),
                              s0 + c2 * (2 * GROUP * MC) + (S_MH + GROUP * MC * u),
                              c0 + c2 * (2 * GROUP * KT) + (C_MOD + GROUP * KT * u),
                              MOD_PIECES, attn_in + cms_in, [s0 + (S_CMS + KT), s0 + (S_CMS + 2 * KT)])

            def adapt(r):
                w0, s0, c0 = r * PC_ROUND + PC_FOLD, r * S_ROUND, r * C_ROUND
                for b in range(GROUP):
                    pe.wait_ge(w_lo, w0 + (PC_ADA + 2 * b + 1))
                    pe.wait_ge(lo_ready, s0 + (S_Z + KT * (b + 1)))
                    for m in range(MC):
                        pe.wait_ge(hi_ready, s0 + (S_Z - GROUP * MC + MC * b + m + 1))
                        tile(bank[MC * b + m][:, :],
                             [(*slot_w(b, 0, k * HC + m * P, k * HC + (m + 1) * P), vc_hi[:, b, k, :], vc_lo[:, b, k, :])
                              for k in range(KT)])
                for b in range(GROUP):
                    pe.wait_ge(w_lo, w0 + (PC_ADA + 2 * b + 2))
                    pe.wait_ge(lo_ready, s0 + (S_AH + MC * (b + 1)))
                    for m in range(KT):
                        if b == 0:
                            pe.wait_ge(acc_added, c0 + (C_UP - KT + m + 1))
                        tile(bank[(4 if b == 0 else 0) + m][:, :],
                             [(*slot_w(b, 1, k * D + m * P, k * D + (m + 1) * P),
                               ph_hi[:, MC * b + k, :], ph_lo[:, MC * b + k, :]) for k in range(MC)])

            for f in range(FOLDS):
                fold(f)
            pe.wait_ge(const_ready, 2)
            attend(0, None)
            with pe.Fori(0, ROUNDS - 1) as r:
                mlp(r)
                adapt(r)
                attend(r + 1, r)
            mlp(ROUNDS - 1)
            adapt(ROUNDS - 1)
            pe.wait_ge(acc_added, C_ROUND * ROUNDS)
            norm_stat(ROUNDS - 1, 0, (4, 5))
            norm_stat(ROUNDS - 1, 1, (6, 7))

        @block.scalar
        def _(act):
            def split_hi(slot, w_at, k, pieces, free_at=None):
                act.wait_ge(mm_done, free_at)
                for q in range(pieces):
                    half = (w_at + (k + q - (k + q) % 2)) // 2
                    act.wait_ge(stage_in[(k + q) % 2], half * 16 + 16)
                    act.activation(ring[:, slot, 0, q, :], stage(k + q), ACT.Copy).then_inc(w_hi, 1)

            def plain_hi(m_at, src, dst, n=KT):
                for m in range(n):
                    act.wait_ge(mm_done, m_at + (m + 1))
                    act.activation(dst(m), src(m), ACT.Copy).then_inc(hi_ready, 1)

            def exps(r, b, m_at, banks):
                for m in range(KT):
                    at = KT * b + m
                    act.wait_ge(nmax_ready, r * (GROUP * KT) + (at + 1))
                    act.activation(pc[:, b, m, :], banks[m][:, :], ACT.Exp, bias=nmax[:, at:at + 1], scale=SCALE,
                                   accum_out=rsum[:, at:at + 1]).then_inc(exp_done, 1)

            def hidden(m_at, s_at, g_at, bias):
                for j in range(GROUP * MC):
                    act.wait_ge(mm_done, m_at + (j + 1))
                    act.wait_ge(lo_ready, s_at + (j - 1))
                    act.sem_inc(act_passed, 1)
                    act.activation(graw[:, j % 2, :], bank[j][:, :], ACT.Gelu, bias=bias(j)).then_inc(raw_ready, 1)
                    act.activation(ph_hi[:, j, :], bank[j][:, :], ACT.Gelu, bias=bias(j)).then_inc(hi_ready, 1)

            def x_split(r_next, free_at):
                g = r_next % 2
                act.wait_ge(mm_done, free_at)
                for n in range(GROUP * KT):
                    act.activation(xa_hi[:, n // KT, n % KT, :], xs_tile(g, n // KT, n % KT), ACT.Copy).then_inc(x_hi, 1)

            def attend(r, before):
                w0, m0, s0 = r * PC_ROUND + PC_FOLD, r * M_ROUND + M_FOLD, r * S_ROUND
                layer = r // 2
                if before is not None:
                    norm_sums(before, 0)
                plain_hi(m0 + M_Y0, lambda m: bank[m][:, :], lambda m: yp_hi[:, m, :])
                if before is not None:
                    norm_squares(before)
                    norm_sums(before, 1)
                plain_hi(m0 + M_V0, lambda m: bank[V0_BANKS[m]][:, :], lambda m: vc_hi[:, 0, m, :])
                exps(r, 0, m0 + M_S0, bank[0:4])
                if before is not None:
                    norm_std(before, (6, 7))
                plain_hi(m0 + M_Y1, lambda m: bank[4 + m][:, :], lambda m: yp_hi[:, m, :])
                split_hi(0, w0, PC_CMS, CMS_PIECES, m0 + M_V1)
                plain_hi(m0 + M_V1, lambda m: bank[m][:, :], lambda m: vc_hi[:, 1, m, :])
                plain_hi(m0 + M_T0, lambda m: bank[4 + m][:, :], lambda m: ph_hi[:, m, :])
                exps(r, 1, m0 + M_S1, bank[0:4])
                for b in range(GROUP):
                    if b == 1:
                        plain_hi(m0 + M_T1, lambda m: bank[m][:, :], lambda m: yp_hi[:, m, :])
                    for m in range(KT):
                        act.wait_ge(mm_done, m0 + ((M_O0, M_O1)[b] + m + 1))
                        act.sem_inc(act_passed, 1)
                        act.activation(xa_hi[:, b, m, :], bank[4 + m][:, :], ACT.Identity,
                                       bias=column(vec, layer, BP + m)).then_inc(hi_ready, 1)

            def mlp(r):
                w0, m0, s0, c0 = r * PC_ROUND + PC_FOLD, r * M_ROUND + M_FOLD, r * S_ROUND, r * C_ROUND
                layer = r // 2

                def chunk(c2, u, per, w_first, m_first, s_first, b_first, pieces_next):
                    m_at = m0 + c2 * (2 * M_CHUNK) + (m_first + M_CHUNK * u)
                    if pieces_next:
                        split_hi(1 - u, w0 + c2 * (2 * per), w_first + per * (u + 1), pieces_next, m_at)
                    hidden(m_at, s0 + c2 * (2 * GROUP * MC) + (s_first + GROUP * MC * u), None,
                           lambda j: column(vec, layer, c2 * (2 * MC) + (b_first + MC * u + j % MC)))

                with act.Fori(0, CH // 2 - 1) as c2:
                    for u in range(2):
                        chunk(c2, u, CMS_PIECES, PC_CMS, M_CMS, S_CH, CB1, CMS_PIECES)
                for u in range(2):
                    chunk(CH // 2 - 1, u, CMS_PIECES, PC_CMS, M_CMS, S_CH, CB1, (CMS_PIECES, MOD_PIECES)[u])
                for n in range(GROUP * KT):
                    act.wait_ge(acc_added, c0 + (C_MOD - GROUP * KT + n + 1))
                    act.activation(vc_hi[:, n // KT, n % KT, :], pc[:, n // KT, n % KT, :], ACT.Identity,
                                   bias=column(cbias, r * 2 + n // KT, n % KT)).then_inc(hi_ready, 1)
                with act.Fori(0, CH // 2 - 1) as c2:
                    for u in range(2):
                        chunk(c2, u, MOD_PIECES, PC_MOD, M_MOD, S_MH, MB1, MOD_PIECES)
                for u in range(2):
                    chunk(CH // 2 - 1, u, MOD_PIECES, PC_MOD, M_MOD, S_MH, MB1, (MOD_PIECES, 2)[u])

            def adapt(r, more):
                w0, m0, s0 = r * PC_ROUND + PC_FOLD, r * M_ROUND + M_FOLD, r * S_ROUND
                split_hi(1, w0, PC_ADA + 2, 2, m0 + M_DOWN)
                g = r % 2
                for n in range(GROUP * KT):
                    act.wait_ge(z_ready, r * (GROUP * KT) + (n + 1))
                    act.activation(vc_hi[:, n // KT, n % KT, :], xs_tile(g, n // KT, n % KT), ACT.Copy).then_inc(hi_ready, 1)
                hidden(m0 + M_DOWN, s0 + S_AH, None, lambda j: column(avec, r * 2 + j // MC, BD + j % MC))
                if more:
                    x_split(r + 1, m0 + M_DOWN)
                    split_hi(0, w0, PC_ROUND + PC_A, 2, m0 + (M_UP + KT))
                    split_hi(1, w0, PC_ROUND + PC_U, 2, m0 + M_ROUND)

            def norm_sums(r, what):
                for b in range(GROUP):
                    act.wait_ge(sum_step, r * 12 + (6 * what + 3 * b + 3))
                    act.activation(ls_hi[:, b, :], lsum[:, b, :], ACT.Copy).then_inc(ls_hi_ready, 1)

            def norm_squares(r):
                g = r % 2
                for n in range(GROUP * KT):
                    act.wait_ge(centred, r * (GROUP * KT) + (n + 1))
                    if n % KT >= 2:
                        act.wait_ge(sum_step, r * 12 + (6 + 3 * (n // KT) + n % KT - 1))
                    elif n >= KT:
                        act.wait_ge(sum_step, r * 12 + (6 + 3))
                    act.sem_inc(act_passed, 1)
                    act.activation(graw[:, n % 2, :], xs_tile(g, n // KT, n % KT), ACT.Square).then_inc(squared, 1)

            def norm_std(r, banks):
                for b in range(GROUP):
                    act.wait_ge(stat_done, r * 4 + (3 + b))
                    act.activation(lsum[:, b, :], bank[banks[b]][:, :], ACT.Sqrt, bias=eps[:, :]).then_inc(std_ready, 1)

            act.dma_start(role_sb[:, :], roles).then_inc(role_in, 16)
            act.dma_start(vec[:, :, :], vecs).then_inc(small_in, 16)
            act.dma_start(code_i[:, :], codes.to_broadcast((P, BATCHES))).then_inc(small_in, 16)
            act.wait_ge(role_in, 16)
            for n in range(BATCHES):
                role = act.value_load(role_sb[0:1, n:n + 1], min_val=0, max_val=ROLES - 1)
                for layer in range(LAYERS):
                    act.dma_start(avec[:, BATCHES * layer + n, :],
                                  avecs[bass.ds(role + ROLES * layer, 1), :, :].rearrange("a p n -> (a p) n")).then_inc(avec_in, 16)

            def fold_hi(f):
                if f >= 2:
                    act.wait_ge(mm_done, KT * (f - 1))
                for q in range(4):
                    act.wait_ge(stage_in[q % 2], 16 * (2 * f + q // 2 + 1))
                    act.activation(fold_piece(f, q)[0], stage(q), ACT.Copy).then_inc(w_hi, 1)

            def fold_copy(f):
                if f >= 2:
                    act.wait_ge(fold_out[f % 2], 16)
                for m in range(KT):
                    act.wait_ge(mm_done, KT * f + m + 1)
                    act.activation(pc[:, f % 2, m, :], bank[4 * (f % 2) + m][:, :], ACT.Copy).then_inc(fold_raw, 1)
                act.wait_ge(fold_raw, KT * (f + 1))
                act.dma_start(folded[f].rearrange("q p n -> p q n"),
                              pc[:, f % 2, :, :].rearrange("p (q k) n -> p q (k n)", q=2)).then_inc(fold_out[f % 2], 16)

            fold_hi(0)
            act.dma_start(xs[:, 0, :, :, :], x_t[0]).then_inc(x_in[0], 16)
            fold_hi(1)
            fold_copy(0)
            fold_hi(2)
            fold_copy(1)
            fold_hi(3)
            act.dma_start(xs[:, 1, :, :, :], x_t[1]).then_inc(x_in[1], 16)
            fold_copy(2)
            act.wait_ge(x_in[0], 16)
            for n in range(GROUP * KT):
                act.activation(xa_hi[:, n // KT, n % KT, :], xs[:, 0, n // KT, n % KT, :], ACT.Copy).then_inc(x_hi, 1)
            fold_copy(3)
            split_hi(0, PC_FOLD, PC_A, 2, M_FOLD)
            split_hi(1, PC_FOLD, PC_U, 2, M_FOLD)
            act.wait_ge(x_in[1], 16)
            act.wait_ge(fold_out[0], 16 * LAYERS)
            act.wait_ge(fold_out[1], 16 * LAYERS)
            act.wait_ge(small_in, 32)
            act.wait_ge(avec_in, 16 * LAYERS * BATCHES)
            act.wait_ge(cbias_ready, LAYERS * BATCHES)
            attend(0, None)
            with act.Fori(0, ROUNDS - 1) as r:
                mlp(r)
                adapt(r, True)
                attend(r + 1, r)
            for n in range(GROUP * KT):
                act.wait_ge(x_final, (ROUNDS - 2) * GROUP * KT + n + 1)
                act.dma_start(out[0, :, n // KT, n % KT, :], xs[:, 0, n // KT, n % KT, :]).then_inc(out_done, 16)
            mlp(ROUNDS - 1)
            adapt(ROUNDS - 1, False)
            norm_sums(ROUNDS - 1, 0)
            norm_squares(ROUNDS - 1)
            norm_sums(ROUNDS - 1, 1)
            norm_std(ROUNDS - 1, (6, 7))
            for n in range(GROUP * KT):
                act.wait_ge(x_final, (ROUNDS - 1) * GROUP * KT + n + 1)
                act.dma_start(out[1, :, n // KT, n % KT, :], xs[:, 1, n // KT, n % KT, :]).then_inc(out_done, 16)
            act.wait_ge(out_done, 16 * 2 * GROUP * KT)

        @block.vector
        def _(dve):
            def split_lo(slot, w_at, k, pieces):
                for q in range(pieces):
                    dve.wait_ge(w_hi, w_at + (k + q + 1))
                    dve.tensor_tensor(ring[:, slot, 1, q, :], stage(k + q), f32(ring[:, slot, 0, q, :]),
                                      ALU.subtract).then_inc(w_lo, 1)

            def plain_lo(s_at, src, hi, lo, n=KT):
                for m in range(n):
                    dve.wait_ge(hi_ready, s_at + (m + 1))
                    dve.tensor_tensor(lo(m), src(m), f32(hi(m)), ALU.subtract).then_inc(lo_ready, 1)

            def softmax(r, b, m_at, banks):
                e0 = r * (GROUP * KT)

                def normalize(m):
                    at = KT * b + m
                    dve.wait_ge(exp_done, e0 + (at + 1))
                    dve.reciprocal(rinv[:, at:at + 1], rsum[:, at:at + 1]).then_inc(rinv_done, 1)
                    dve.wait_ge(rinv_done, e0 + (at + 1))
                    dve.tensor_scalar(pc[:, b, m, :], pc[:, b, m, :], rinv[:, at:at + 1], None, ALU.mult).then_inc(p_ready, 1)

                for m in range(KT):
                    at = KT * b + m
                    dve.wait_ge(mm_done, m_at + (m + 1))
                    dve.reduce_max(smax[:, at:at + 1], banks[m][:, :], AX.X).then_inc(smax_done, 1)
                    dve.wait_ge(smax_done, e0 + (at + 1))
                    dve.tensor_scalar(nmax[:, at:at + 1], smax[:, at:at + 1], -SCALE, None, ALU.mult).then_inc(nmax_ready, 1)
                    if m:
                        normalize(m - 1)
                normalize(KT - 1)

            def zero(b):
                for m in range(KT):
                    dve.memset(pc[:, b, m, :], 0.0).then_inc(acc_added, 1)

            def attend(r, before):
                w0, m0, s0 = r * PC_ROUND + PC_FOLD, r * M_ROUND + M_FOLD, r * S_ROUND
                layer = r // 2
                if before is not None:
                    norm_sums(before)
                plain_lo(s0 + S_Y0, lambda m: bank[m][:, :], lambda m: yp_hi[:, m, :], lambda m: yp_lo[:, m, :])
                if before is not None:
                    norm_centre(before, (4, 5))
                    norm_square_sums(before)
                plain_lo(s0 + S_V0, lambda m: bank[V0_BANKS[m]][:, :], lambda m: vc_hi[:, 0, m, :], lambda m: vc_lo[:, 0, m, :])
                softmax(r, 0, m0 + M_S0, bank[0:4])
                plain_lo(s0 + S_Y1, lambda m: bank[4 + m][:, :], lambda m: yp_hi[:, m, :], lambda m: yp_lo[:, m, :])
                split_lo(0, w0, PC_CMS, CMS_PIECES)
                plain_lo(s0 + S_V1, lambda m: bank[m][:, :], lambda m: vc_hi[:, 1, m, :], lambda m: vc_lo[:, 1, m, :])
                plain_lo(s0 + S_P0, lambda m: bank[4 + m][:, :], lambda m: ph_hi[:, m, :], lambda m: ph_lo[:, m, :])
                softmax(r, 1, m0 + M_S1, bank[0:4])
                for b in range(GROUP):
                    if b == 1:
                        plain_lo(s0 + S_P1, lambda m: bank[m][:, :], lambda m: yp_hi[:, m, :], lambda m: yp_lo[:, m, :])
                    for m in range(KT):
                        dve.wait_ge(hi_ready, s0 + ((S_O0, S_O1)[b] + m + 1))
                        dve.scalar_tensor_tensor(xa_lo[:, b, m, :], bank[4 + m][:, :], column(vec, layer, BP + m),
                                                 f32(xa_hi[:, b, m, :]), ALU.add, ALU.subtract).then_inc(lo_ready, 1)
                    zero(b)
                if before is not None:
                    norm_scale(before)

            def mlp(r):
                w0, m0, s0, c0 = r * PC_ROUND + PC_FOLD, r * M_ROUND + M_FOLD, r * S_ROUND, r * C_ROUND
                g = r % 2

                def chunk(c2, u, per, w_first, m_first, s_first, c_first, pieces_next, acc):
                    if pieces_next:
                        split_lo(1 - u, w0 + c2 * (2 * per), w_first + per * (u + 1), pieces_next)
                    s_at = s0 + c2 * (2 * GROUP * MC) + (s_first + GROUP * MC * u)
                    plain_lo(s_at, lambda j: graw[:, j % 2, :], lambda j: ph_hi[:, j, :], lambda j: ph_lo[:, j, :], GROUP * MC)
                    m_at = m0 + c2 * (2 * M_CHUNK) + (m_first + M_CHUNK * u + GROUP * MC)
                    c_at = c0 + c2 * (2 * GROUP * KT) + (c_first + GROUP * KT * u)
                    for n in range(GROUP * KT):
                        dve.wait_ge(mm_done, m_at + (n + 1))
                        dve.wait_ge(acc_added, c_at + (n - 7))
                        dve.tensor_tensor(acc(n), acc(n), bank[4 + n % KT][:, :], ALU.add).then_inc(acc_added, 1)

                def cms_acc(n):
                    return pc[:, n // KT, n % KT, :]

                def mod_acc(n):
                    return xs_tile(g, n // KT, n % KT)

                with dve.Fori(0, CH // 2 - 1) as c2:
                    for u in range(2):
                        chunk(c2, u, CMS_PIECES, PC_CMS, M_CMS, S_CH, C_CMS, CMS_PIECES, cms_acc)
                for u in range(2):
                    chunk(CH // 2 - 1, u, CMS_PIECES, PC_CMS, M_CMS, S_CH, C_CMS, (CMS_PIECES, MOD_PIECES)[u], cms_acc)
                for n in range(GROUP * KT):
                    b, k = n // KT, n % KT
                    dve.wait_ge(hi_ready, s0 + (S_CMS + n + 1))
                    dve.scalar_tensor_tensor(vc_lo[:, b, k, :], pc[:, b, k, :], column(cbias, r * 2 + b, k),
                                             f32(vc_hi[:, b, k, :]), ALU.add, ALU.subtract).then_inc(lo_ready, 1)
                for n in range(GROUP * KT):
                    b, k = n // KT, n % KT
                    dve.scalar_tensor_tensor(xs_tile(g, b, k), pc[:, b, k, :], column(cbias, r * 2 + b, k),
                                             xs_tile(g, b, k), ALU.add, ALU.add).then_inc(res_added, 1)
                dve.wait_ge(res_added, r * (GROUP * KT) + GROUP * KT)
                dve.sem_inc(dve_passed, 1)
                with dve.Fori(0, CH // 2 - 1) as c2:
                    for u in range(2):
                        chunk(c2, u, MOD_PIECES, PC_MOD, M_MOD, S_MH, C_MOD, MOD_PIECES, mod_acc)
                for u in range(2):
                    chunk(CH // 2 - 1, u, MOD_PIECES, PC_MOD, M_MOD, S_MH, C_MOD, (MOD_PIECES, 2)[u], mod_acc)

            def adapt(r, more):
                w0, m0, s0, c0, e0 = (r * PC_ROUND + PC_FOLD, r * M_ROUND + M_FOLD, r * S_ROUND, r * C_ROUND,
                                      r * (GROUP * KT))
                g, layer = r % 2, r // 2
                split_lo(1, w0, PC_ADA + 2, 2)
                for b in range(GROUP):
                    for k in range(KT):
                        n = KT * b + k
                        dve.wait_ge(acc_added, c0 + (C_UP - GROUP * KT + n + 1))
                        dve.tensor_scalar(xs_tile(g, b, k), xs_tile(g, b, k), column(vec, layer, MB2 + k), 0.0,
                                          ALU.add, ALU.max).then_inc(z_low, 1)
                    for k in range(KT):
                        n = KT * b + k
                        dve.wait_ge(z_low, e0 + (n + 1))
                        dve.tensor_scalar(xs_tile(g, b, k), xs_tile(g, b, k), 1.0, None, ALU.min).then_inc(z_ready, 1)
                    plain_lo(s0 + (S_Z + KT * b), lambda k: xs_tile(g, b, k), lambda k: vc_hi[:, b, k, :],
                             lambda k: vc_lo[:, b, k, :])
                plain_lo(s0 + S_AH, lambda j: graw[:, j % 2, :], lambda j: ph_hi[:, j, :], lambda j: ph_lo[:, j, :], GROUP * MC)
                if more:
                    for n in range(GROUP * KT):
                        dve.wait_ge(x_hi, e0 + (GROUP * KT + n + 1))
                        dve.tensor_tensor(xa_lo[:, n // KT, n % KT, :], xs_tile((r + 1) % 2, n // KT, n % KT),
                                          f32(xa_hi[:, n // KT, n % KT, :]), ALU.subtract).then_inc(x_lo, 1)
                for b in range(GROUP):
                    for k in range(KT):
                        n = KT * b + k
                        dve.wait_ge(mm_done, m0 + (M_UP + n + 1))
                        dve.scalar_tensor_tensor(xs_tile(g, b, k), bank[(4 if b == 0 else 0) + k][:, :],
                                                 column(avec, r * 2 + b, BU + k), xs_tile(g, b, k),
                                                 ALU.add, ALU.add).then_inc(acc_added, 1)
                    if more:
                        split_lo(b, w0, PC_ROUND + (PC_A, PC_U)[b], 2)

            def norm_sum3(r, what, b, terms, ready):
                at = r * 12 + (6 * what + 3 * b)
                for n in range(3):
                    if ready:
                        ready(n)
                    if n:
                        dve.wait_ge(sum_step, at + n)
                    dve.tensor_tensor(lsum[:, b, :], lsum[:, b, :] if n else terms(0), terms(n + 1),
                                      ALU.add).then_inc(sum_step, 1)

            def norm_lo(r, what):
                for b in range(GROUP):
                    dve.wait_ge(ls_hi_ready, r * 4 + (2 * what + b + 1))
                    dve.tensor_tensor(ls_lo[:, b, :], lsum[:, b, :], f32(ls_hi[:, b, :]), ALU.subtract).then_inc(ls_lo_ready, 1)

            def norm_sums(r):
                g = r % 2
                dve.wait_ge(acc_added, r * C_ROUND + C_ROUND)
                for b in range(GROUP):
                    norm_sum3(r, 0, b, lambda k: xs_tile(g, b, k), None)
                norm_lo(r, 0)

            def norm_centre(r, banks):
                g = r % 2
                for b in range(GROUP):
                    dve.wait_ge(stat_done, r * 4 + (b + 1))
                    for k in range(KT):
                        dve.tensor_tensor(xs_tile(g, b, k), xs_tile(g, b, k), bank[banks[b]][:, :],
                                          ALU.subtract).then_inc(centred, 1)

            def norm_square_sums(r):
                for b in range(GROUP):
                    norm_sum3(r, 1, b, lambda k: graw[:, k % 2, :],
                              lambda n: dve.wait_ge(squared, r * (GROUP * KT) + (KT * b + n + 2)))
                norm_lo(r, 1)

            def norm_scale(r):
                g = r % 2
                for b in range(GROUP):
                    dve.wait_ge(std_ready, r * GROUP + (b + 1))
                    dve.reciprocal(lsum[:, b, :], lsum[:, b, :]).then_inc(rstd_ready, 1)
                for b in range(GROUP):
                    dve.wait_ge(rstd_ready, r * GROUP + (b + 1))
                    for k in range(KT):
                        dve.tensor_tensor(xs_tile(g, b, k), xs_tile(g, b, k), lsum[:, b, :], ALU.mult).then_inc(scaled, 1)
                    for k in range(KT):
                        dve.wait_ge(scaled, r * (GROUP * KT) + (KT * b + k + 1))
                        dve.tensor_scalar(xs_tile(g, b, k), xs_tile(g, b, k), column(avec, r * 2 + b, GA + k),
                                          column(avec, r * 2 + b, BE + k), ALU.mult, ALU.add).then_inc(x_final, 1)

            dve.wait_ge(iota_ready, 2)
            dve.tensor_copy(mean_w[:, :], ones[:, :]).then_inc(code_ready, 1)
            dve.tensor_copy(feat_f[:, :], feat_i[:, :]).then_inc(code_ready, 1)
            dve.wait_ge(small_in, 32)
            dve.tensor_copy(code_f[:, :], code_i[:, :]).then_inc(code_ready, 1)
            dve.wait_ge(code_ready, 3)
            dve.tensor_scalar(mean_w[:, :], f32(mean_w[:, :]), 1.0 / D, None, ALU.mult).then_inc(const_ready, 1)
            for n in range(BATCHES):
                dve.tensor_scalar(hot[:, n, :], feat_f[:, :], code_f[:, n:n + 1], None, ALU.is_equal).then_inc(hot_ready, 1)
            dve.wait_ge(hot_ready, BATCHES)
            for layer in range(LAYERS):
                for n in range(BATCHES):
                    dve.tensor_tensor(cbias[:, BATCHES * layer + n, :], hot[:, n, :], vec[:, layer, CB2:CB2 + KT],
                                      ALU.add).then_inc(cbias_ready, 1)

            def fold_lo(f):
                for q in range(4):
                    dve.wait_ge(w_hi, 4 * f + q + 1)
                    hi, lo = fold_piece(f, q)
                    dve.tensor_tensor(lo, stage(q), f32(hi), ALU.subtract).then_inc(w_lo, 1)

            for f in range(FOLDS):
                fold_lo(f)
            for n in range(GROUP * KT):
                dve.wait_ge(x_hi, n + 1)
                dve.tensor_tensor(xa_lo[:, n // KT, n % KT, :], xs[:, 0, n // KT, n % KT, :],
                                  f32(xa_hi[:, n // KT, n % KT, :]), ALU.subtract).then_inc(x_lo, 1)
            split_lo(0, PC_FOLD, PC_A, 2)
            split_lo(1, PC_FOLD, PC_U, 2)
            dve.wait_ge(avec_in, 16 * LAYERS * BATCHES)
            dve.wait_ge(cbias_ready, LAYERS * BATCHES)
            attend(0, None)
            with dve.Fori(0, ROUNDS - 1) as r:
                mlp(r)
                adapt(r, True)
                attend(r + 1, r)
            mlp(ROUNDS - 1)
            adapt(ROUNDS - 1, False)
            norm_sums(ROUNDS - 1)
            norm_centre(ROUNDS - 1, (4, 5))
            norm_square_sums(ROUNDS - 1)
            norm_scale(ROUNDS - 1)


def _tiles(w, cols=None):
    n = w.shape[0] // P
    return w.reshape(n, P, w.shape[1]).transpose(1, 0, 2).reshape(P, n * w.shape[1])


def _pieces(a):
    return a.reshape(P, -1, PIECE).transpose(1, 0, 2)


def _vector(v):
    return v.reshape(-1, P).T


def kernel(**inputs):
    import concourse.bacc as bacc
    from concourse.bass_utils import run_bass_kernel_spmd

    a = {k: np.asarray(v) for k, v in inputs.items()}
    cond, ada = ("L0_cond_", "L2_cond_"), ("L1_cond_", "L3_cond_")
    down_up = [("W_down", "b_down", "W_up", "b_up", "gamma", "beta"), ("W_down", "b_down", "W_up", "b_up", "ln_w", "ln_b")]

    x_t = a["x"].reshape(2, GROUP, T, KT, P).transpose(0, 4, 1, 3, 2)
    fold_w, cms_w, mod_w, vecs = [], [], [], []
    for p in cond:
        for left, right in ((a[p + "Wq"].T, a[p + "Wk"].T), (a[p + "Wv"].T, a[p + "Wp"])):
            fold_w += [_pieces(_tiles(left)), _pieces(_tiles(right))]
        for c in range(CH):
            s = slice(c * HC, (c + 1) * HC)
            cms_w += [_pieces(_tiles(a[p + "cW1"][:, s])), _pieces(_tiles(a[p + "cW2"][s]))]
            mod_w += [_pieces(_tiles(a[p + "mW1"][:, s])), _pieces(_tiles(a[p + "mW2"][s]))]
        vecs.append(np.concatenate([_vector(a[p + n]) for n in ("bp", "cb1", "cb2", "mb1", "mb2")], 1))
    ada_w, avecs = [], []
    for p, (wd, bd, wu, bu, ga, be) in zip(ada, down_up):
        for role in range(ROLES):
            ada_w += [_pieces(_tiles(a[p + wd][role])), _pieces(_tiles(a[p + wu][role]))]
            avecs.append(np.concatenate([_vector(a[p + n][role]) for n in (bd, bu, ga, be)], 1))
    arrays = {
        "x_t": x_t,
        "codes": a["itok_B_17_1546"].reshape(1, BATCHES),
        "roles": a["itok_B_1_2"].reshape(1, BATCHES),
        "fold_w": np.concatenate(fold_w), "cms_w": np.concatenate(cms_w), "mod_w": np.concatenate(mod_w),
        "ada_w": np.concatenate(ada_w),
        "vecs": np.stack(vecs).transpose(1, 0, 2), "avecs": np.stack(avecs),
    }
    arrays = {k: np.ascontiguousarray(v) for k, v in arrays.items()}
    nc = bacc.Bacc("TRN2", target_bir_lowering=False, num_devices=1, dynamic_dma_scratch_size=1024)
    args = [nc.dram_tensor(k, v.shape, mybir.dt.from_np(v.dtype), kind="ExternalInput").ap() for k, v in arrays.items()]
    out = nc.dram_tensor("out", (2, P, GROUP, KT, T), F32, kind="ExternalOutput").ap()
    build(nc, *args, out)
    got = run_bass_kernel_spmd(nc, [arrays], core_ids=[0]).results[0]["out"]
    return got.transpose(0, 2, 4, 3, 1).reshape(BATCHES, T, D)
```

```python
from contextlib import ExitStack

import numpy as np
import concourse.bass as bass
from concourse import mybir

F32, F32R, I32 = mybir.dt.float32, mybir.dt.float32r, mybir.dt.int32
ACT, ALU, AX = mybir.ActivationFunctionType, mybir.AluOpType, mybir.AxisListType

P = 128
D = 512
T = 512
KT = D // P
HID = 2048
HC = 256
MC = HC // P
CH = HID // HC
BATCHES, GROUP, LAYERS, ROLES = 4, 2, 2, 3
ROUNDS = LAYERS * BATCHES // GROUP
EPS = 1e-5
SCALE = float(D) ** -0.5
PIECE = 1024

BP, CB1, CB2, MB1, MB2 = 0, KT, KT + HID // P, 2 * KT + HID // P, 2 * KT + 2 * HID // P
NVEC = 3 * KT + 2 * HID // P
BD, BU, GA, BE = 0, MC, MC + KT, MC + 2 * KT
NAVEC = MC + 3 * KT

CMS_PIECES, MOD_PIECES = 2, 3
PC_A, PC_U = 0, 2
PC_CMS = 4
PC_MOD = PC_CMS + CMS_PIECES * CH
PC_ADA = PC_MOD + MOD_PIECES * CH
PC_ROUND = PC_ADA + 2 * GROUP
FOLDS = 2 * LAYERS
PC_FOLD = 4 * FOLDS

M_Y0, M_V0, M_S0, M_Y1, M_V1, M_T0, M_S1 = range(0, 28, KT)
M_O0, M_T1, M_O1 = (28, 29, 34, 35), 30, (36, 37, 38, 39)
M_CMS = 40
M_CHUNK = GROUP * (MC + KT)
M_MOD = M_CMS + M_CHUNK * CH
M_DOWN = M_MOD + M_CHUNK * CH
M_UP = M_DOWN + GROUP * MC
M_ROUND = M_UP + GROUP * KT
M_FOLD = FOLDS * KT

S_Y0, S_V0, S_Y1, S_V1, S_P0 = range(0, 20, KT)
S_O0, S_P1, S_O1 = (20, 21, 26, 27), 22, (28, 29, 30, 31)
S_CH = 32
S_CMS = S_CH + GROUP * MC * CH
S_MH = S_CMS + GROUP * KT
S_Z = S_MH + GROUP * MC * CH
S_AH = S_Z + GROUP * KT
S_ROUND = S_AH + GROUP * MC

C_CMS = GROUP * KT
C_MOD = C_CMS + GROUP * KT * CH
C_UP = C_MOD + GROUP * KT * CH
C_ROUND = C_UP + GROUP * KT

V0_BANKS = (6, 7, 4, 5)


def build(nc, x_t, codes, roles, fold_w, cms_w, mod_w, ada_w, vecs, avecs, out):
    folded = nc.dram_tensor("folded", (FOLDS, 2, P, PIECE), F32, kind="Internal").ap()
    ctx = ExitStack()
    with ctx:
        def sb(name, shape, dt=F32):
            return ctx.enter_context(nc.sbuf_tensor(name, shape, dt))

        def sem(name):
            return ctx.enter_context(nc.semaphore(name))

        xs = sb("xs", [P, 2, GROUP, KT, T])
        xa_hi, xa_lo = (sb(f"xa_{n}", [P, GROUP, KT, T], F32R) for n in ("hi", "lo"))
        vc_hi, vc_lo = (sb(f"vc_{n}", [P, GROUP, KT, T], F32R) for n in ("hi", "lo"))
        yp_hi, yp_lo = (sb(f"yp_{n}", [P, KT, T], F32R) for n in ("hi", "lo"))
        ph_hi, ph_lo = (sb(f"ph_{n}", [P, KT, T], F32R) for n in ("hi", "lo"))
        pc = sb("pc", [P, GROUP, KT, T])
        ring = sb("ring", [P, 2, 2, 3, PIECE], F32R)
        staging = sb("staging", [P, 2, PIECE])
        graw = sb("graw", [P, 2, T])
        lsum = sb("lsum", [P, GROUP, T])
        ls_hi, ls_lo = (sb(f"ls_{n}", [P, GROUP, T], F32R) for n in ("hi", "lo"))
        ident = sb("ident", [P, P])
        mean_w = sb("mean_w", [P, P], F32R)
        mean_f = sb("mean_f", [P, P])
        vec = sb("vec", [P, LAYERS, NVEC])
        avec = sb("avec", [P, LAYERS * BATCHES, NAVEC])
        cbias = sb("cbias", [P, LAYERS * BATCHES, KT])
        xbias = sb("xbias", [P, LAYERS * BATCHES, KT])
        code_i = sb("code_i", [P, BATCHES], I32)
        code_f = sb("code_f", [P, BATCHES])
        role_sb = sb("role_sb", [1, BATCHES], I32)
        feat_i = sb("feat_i", [P, KT], I32)
        feat_f = sb("feat_f", [P, KT])
        hot = sb("hot", [P, BATCHES, KT])
        eps = sb("eps", [P, 1])
        smax = sb("smax", [P, GROUP * KT])
        nmax = sb("nmax", [P, GROUP * KT])
        rsum = sb("rsum", [P, GROUP * KT])
        rinv = sb("rinv", [P, GROUP * KT])
        bank = [ctx.enter_context(nc.psum_tensor(f"bank{i}", [P, 512], F32)) for i in range(8)]

        stage_in = [sem("stage_in0"), sem("stage_in1")]
        w_hi, w_lo = sem("w_hi"), sem("w_lo")
        mm_done = sem("mm_done")
        hi_ready, lo_ready = sem("hi_ready"), sem("lo_ready")
        x_hi, x_lo = sem("x_hi"), sem("x_lo")
        fold_in = [sem(f"fold_in{i}") for i in range(4)]
        fold_raw = sem("fold_raw")
        fold_out = [sem("fold_out0"), sem("fold_out1")]
        x_in = [sem("x_in0"), sem("x_in1")]
        small_in, role_in, avec_in = sem("small_in"), sem("role_in"), sem("avec_in")
        const_ready, iota_ready, code_ready, hot_ready, cbias_ready, xbias_ready = (
            sem(n) for n in ("const_ready", "iota_ready", "code_ready", "hot_ready", "cbias_ready", "xbias_ready"))
        smax_done, nmax_ready, exp_done, rinv_done, p_ready = (
            sem(n) for n in ("smax_done", "nmax_ready", "exp_done", "rinv_done", "p_ready"))
        raw_ready, acc_added, res_added, z_ready = (
            sem(n) for n in ("raw_ready", "acc_added", "res_added", "z_ready"))
        sum_step, ls_hi_ready, ls_lo_ready, stat_done, centred, squared, std_ready, rstd_ready, scaled, x_final = (
            sem(n) for n in ("sum_step", "ls_hi_ready", "ls_lo_ready", "stat_done", "centred", "squared",
                             "std_ready", "rstd_ready", "scaled", "x_final"))
        out_done = sem("out_done")
        sp_passed, act_passed, dve_passed = sem("sp_passed"), sem("act_passed"), sem("dve_passed")

        def fold_places(f):
            if f % 2 == 0:
                return (vc_hi[:, 0], vc_lo[:, 0]), (vc_hi[:, 1], vc_lo[:, 1])
            return (yp_hi[:, :, :], yp_lo[:, :, :]), (ph_hi[:, :, :], ph_lo[:, :, :])

        def fold_piece(f, q):
            part = fold_places(f)[q // 2]
            return [x[:, 2 * (q % 2):2 * (q % 2) + 2, :].rearrange("p k n -> p (k n)") for x in part]

        def stage(q):
            return staging[:, q % 2, :]

        FOLD_ORDER = (0, 2, 1, 3)

        def fold_stage(n):
            return xs[:, 1, n // 2, 2 * (n % 2):2 * (n % 2) + 2, :].rearrange("p k n -> p (k n)")

        def f32(ap):
            return ap.bitcast(F32)

        def xs_tile(g, b, k):
            if isinstance(g, int):
                return xs[:, g, b, k, :]
            return xs[:, bass.ds(g, 1), b, k, :].rearrange("p a n -> p (a n)")

        def column(t, row, c):
            width = t.shape[2]
            flat = t[:, :, :].rearrange("p r c -> p (r c)")
            at = row * width + c
            return flat[:, at:at + 1] if isinstance(at, int) else flat[:, bass.ds(at, 1)]

        block = ctx.enter_context(nc.Block())

        @block.sync
        def _(sp):
            def load(src, free_at, k):
                sp.wait_ge(w_lo, free_at)
                sp.dma_start(stage(k), src).then_inc(stage_in[k % 2], 16)

            for q in range(PC_FOLD):
                if q >= 4:
                    sp.wait_ge(w_lo, q - 3)
                sp.dma_start(fold_stage(q % 4), fold_w[q - q % 4 + FOLD_ORDER[q % 4]]).then_inc(fold_in[q % 4], 16)

            with sp.Fori(0, ROUNDS) as r:
                base = r * PC_ROUND + PC_FOLD
                layer = r // 2
                for w in range(2):
                    sp.wait_ge(fold_out[w], layer * 16 + 16)
                    sp.sem_inc(sp_passed, 1)
                    for q in range(2):
                        src = folded[bass.ds(layer * 2 + w, 1), q, :, :].rearrange("a p n -> (a p) n")
                        load(src, base + (2 * w + q - 1), q)
                with sp.Fori(0, CH) as c:
                    for q in range(CMS_PIECES):
                        src = cms_w[bass.ds(layer * (CMS_PIECES * CH) + c * CMS_PIECES + q, 1), :, :].rearrange("a p n -> (a p) n")
                        load(src, base + c * CMS_PIECES + (PC_CMS + q - 1), q)
                with sp.Fori(0, CH // 2) as c2:
                    for q in range(2 * MOD_PIECES):
                        src = mod_w[bass.ds(layer * (MOD_PIECES * CH) + c2 * (2 * MOD_PIECES) + q, 1), :, :].rearrange("a p n -> (a p) n")
                        load(src, base + c2 * (2 * MOD_PIECES) + (PC_MOD + q - 1), q)
                sp.wait_ge(role_in, 16)
                for b in range(GROUP):
                    role = sp.value_load(role_sb[0:1, bass.ds((r % 2) * GROUP + b, 1)], min_val=0, max_val=ROLES - 1)
                    for q in range(2):
                        src = ada_w[bass.ds((layer * ROLES + role) * 2 + q, 1), :, :].rearrange("a p n -> (a p) n")
                        load(src, base + (PC_ADA + 2 * b + q - 1), q)
            for g in range(2):
                for n in range(GROUP * KT):
                    sp.wait_ge(x_final, (ROUNDS - 2 + g) * GROUP * KT + n + 1)
                    sp.dma_start(out[g, :, n // KT, n % KT, :], xs[:, g, n // KT, n % KT, :]).then_inc(out_done, 16)
            sp.wait_ge(out_done, 16 * 2 * GROUP * KT)

        @block.gpsimd
        def _(pool):
            pool.memset(ident[:, :], 0.0).then_inc(iota_ready, 1)
            pool.memset(mean_f[:, :], 1.0 / D)
            pool.memset(eps[:, :], EPS)
            pool.iota(feat_i[:, :], pattern=[[P, KT]], base=0, channel_multiplier=1).then_inc(iota_ready, 1)
            pool.wait_ge(iota_ready, 1)
            pool.affine_select(out=ident[:, :], in_=ident[:, :], compare_op=ALU.not_equal, fill=1.0,
                               base=0, pattern=[[-1, P]], channel_multiplier=1).then_inc(const_ready, 1)
            pool.dma_start(role_sb[:, :], roles).then_inc(role_in, 16)
            pool.dma_start(vec[:, :, :], vecs).then_inc(small_in, 16)
            pool.dma_start(code_i[:, :], codes.to_broadcast((P, BATCHES))).then_inc(small_in, 16)
            pool.wait_ge(role_in, 16)
            for n in range(BATCHES):
                role = pool.value_load(role_sb[0:1, n:n + 1], min_val=0, max_val=ROLES - 1)
                for layer in range(LAYERS):
                    pool.dma_start(avec[:, BATCHES * layer + n, :],
                                  avecs[bass.ds(role + ROLES * layer, 1), :, :].rearrange("a p n -> (a p) n")).then_inc(avec_in, 16)

        @block.tensor
        def _(pe):
            def tile(dst, parts, ready=None):
                last = len(parts) - 1
                for n, (lh, ll, rh, rl) in enumerate(parts):
                    if ready:
                        ready(n)
                    pe.matmul(dst, lh, rh, start=n == 0, stop=False)
                    pe.matmul(dst, lh, rl, start=False, stop=False)
                    done = pe.matmul(dst, ll, rh, start=False, stop=n == last)
                return done.then_inc(mm_done, 1)

            def slot_w(slot, piece, lo, hi):
                return ring[:, slot, 0, piece, lo:hi], ring[:, slot, 1, piece, lo:hi]

            def fold(f):
                (lh, ll), (rh, rl) = fold_places(f)
                for m in range(KT):
                    if f >= 2:
                        pe.wait_ge(fold_raw, 4 * (f - 2) + m + 1)
                    tile(bank[4 * (f % 2) + m][:, :],
                         [(lh[:, k, m * P:(m + 1) * P], ll[:, k, m * P:(m + 1) * P], rh[:, k, :], rl[:, k, :])
                          for k in range(KT)],
                         (lambda k: pe.wait_ge(w_lo, 4 * f + 2 + k // 2 * 2)) if m == 0 else None)

            def project_y(b, m, dst):
                tile(dst, [(*slot_w(0, k // 2, (k % 2) * D + m * P, (k % 2) * D + (m + 1) * P),
                            xa_hi[:, b, k, :], xa_lo[:, b, k, :]) for k in range(KT)])

            def project_v(b, m, dst):
                tile(dst, [(xa_hi[:, b, k, m * P:(m + 1) * P], xa_lo[:, b, k, m * P:(m + 1) * P],
                            *slot_w(1, k // 2, (k % 2) * D, (k % 2 + 1) * D)) for k in range(KT)])

            def scores(b, m, dst):
                tile(dst, [(yp_hi[:, k, m * P:(m + 1) * P], yp_lo[:, k, m * P:(m + 1) * P],
                            xa_hi[:, b, k, :], xa_lo[:, b, k, :]) for k in range(KT)])

            def transposed(b, j, dst):
                for i in range(KT):
                    done = pe.transpose(dst[:, i * P:(i + 1) * P], pc[:, b, i, j * P:(j + 1) * P], ident[:, :])
                done.then_inc(mm_done, 1)

            def attended(b, m, dst, p_hi, p_lo, ready=None):
                tile(dst, [(vc_hi[:, b, k, m * P:(m + 1) * P], vc_lo[:, b, k, m * P:(m + 1) * P],
                            p_hi[:, k, :], p_lo[:, k, :]) for k in range(KT)], ready)

            def stat(dst, b):
                pe.matmul(dst, mean_w[:, :], ls_hi[:, b, :], start=True, stop=False)
                pe.matmul(dst, mean_w[:, :], ls_lo[:, b, :], start=False, stop=True).then_inc(stat_done, 1)

            def norm_stat(r, what, banks):
                for b in range(GROUP):
                    pe.wait_ge(ls_lo_ready, r * 4 + (2 * what + b + 1))
                    stat(bank[banks[b]][:, :], b)

            def attend(r, before):
                w0, s0, e0 = r * PC_ROUND + PC_FOLD, r * S_ROUND, r * (GROUP * KT)
                pe.wait_ge(w_lo, w0 + (PC_A + 2))
                pe.wait_ge(x_lo, e0 + KT)
                for m in range(KT):
                    if before is None:
                        pe.wait_ge(fold_raw, 8 + m + 1)
                    else:
                        pe.wait_ge(acc_added, before * C_ROUND + (C_UP + KT + m + 1))
                    project_y(0, m, bank[m][:, :])
                if before is not None:
                    norm_stat(before, 0, (4, 5))
                pe.wait_ge(w_lo, w0 + (PC_U + 2))
                for m in range(KT):
                    if before is None:
                        pe.wait_ge(fold_raw, 12 + KT)
                    elif m >= 2:
                        pe.wait_ge(centred, before * (GROUP * KT) + (m - 1) * KT)
                    project_v(0, m, bank[V0_BANKS[m]][:, :])
                pe.wait_ge(lo_ready, s0 + (S_Y0 + KT))
                for m in range(KT):
                    scores(0, m, bank[m][:, :])
                if before is not None:
                    pe.wait_ge(lo_ready, s0 + (S_V0 + 2))
                    norm_stat(before, 1, (6, 7))
                pe.wait_ge(x_lo, e0 + 2 * KT)
                pe.wait_ge(lo_ready, s0 + (S_V0 + KT))
                for m in range(KT):
                    if before is not None and m >= 2:
                        pe.wait_ge(std_ready, before * GROUP + (m - 1))
                    project_y(1, m, bank[4 + m][:, :])
                for m in range(KT):
                    pe.wait_ge(exp_done, e0 + (m + 1))
                    project_v(1, m, bank[m][:, :])
                pe.wait_ge(p_ready, e0 + KT)
                for m in range(KT):
                    pe.wait_ge(lo_ready, s0 + (S_Y1 + m + 1))
                    transposed(0, m, bank[4 + m])
                for m in range(KT):
                    pe.wait_ge(lo_ready, s0 + (S_V1 + m + 1))
                    scores(1, m, bank[m][:, :])
                pe.wait_ge(lo_ready, s0 + (S_P0 + KT))
                for m in range(2):
                    attended(0, m, bank[4 + m][:, :], ph_hi, ph_lo)
                pe.wait_ge(p_ready, e0 + 2 * KT)
                for m in range(KT):
                    transposed(1, m, bank[m])
                for m in range(2, KT):
                    attended(0, m, bank[4 + m][:, :], ph_hi, ph_lo)
                for m in range(KT):
                    pe.wait_ge(lo_ready, s0 + (S_O0[m] + 1))
                    attended(1, m, bank[4 + m][:, :], yp_hi, yp_lo,
                             (lambda k: pe.wait_ge(lo_ready, s0 + (S_P1 + k + 1))) if m == 0 else None)

            def chunk(slot, w_at, h_at, c_at, pieces, inputs, inputs_ready):
                up = pieces - 1
                per = KT if up == 1 else 4
                pe.wait_ge(w_lo, w_at + up)
                for b in range(GROUP):
                    for m in range(MC):
                        pe.wait_ge(hi_ready, h_at + (MC * b + m - 3))
                        tile(bank[MC * b + m][:, :],
                             [(*slot_w(slot, k // per, (k % per) * HC + m * P, (k % per) * HC + (m + 1) * P),
                               *(x[:, b, kk, :] for x in pair))
                              for k, (pair, kk) in enumerate(inputs)],
                             (lambda k: inputs_ready(b, k)) if m == 0 else None)
                pe.wait_ge(w_lo, w_at + pieces)
                for b in range(GROUP):
                    pe.wait_ge(lo_ready, h_at + (MC * b + MC))
                    for m in range(KT):
                        pe.wait_ge(acc_added, c_at + (KT * b + m - 3))
                        tile(bank[4 + m][:, :],
                             [(*slot_w(slot, up, k * D + m * P, k * D + (m + 1) * P),
                               ph_hi[:, MC * b + k, :], ph_lo[:, MC * b + k, :]) for k in range(MC)])

            attn_in = [((xa_hi, xa_lo), k) for k in range(KT)]
            cms_in = [((vc_hi, vc_lo), k) for k in range(KT)]

            def mlp(r):
                w0, s0, c0 = r * PC_ROUND + PC_FOLD, r * S_ROUND, r * C_ROUND

                def attn_ready(b, k):
                    if k == 0:
                        pe.wait_ge(lo_ready, s0 + ((S_O0, S_O1)[b][KT - 1] + 1))

                def cms_ready(b, k):
                    if k == KT:
                        pe.wait_ge(lo_ready, s0 + (S_CMS + KT * (b + 1)))

                with pe.Fori(0, CH // 2) as c2:
                    for u in range(2):
                        chunk(u, w0 + c2 * (2 * CMS_PIECES) + (PC_CMS + CMS_PIECES * u),
                              s0 + c2 * (2 * GROUP * MC) + (S_CH + GROUP * MC * u),
                              c0 + c2 * (2 * GROUP * KT) + (C_CMS + GROUP * KT * u),
                              CMS_PIECES, attn_in, attn_ready)
                with pe.Fori(0, CH // 2) as c2:
                    for u in range(2):
                        chunk(u, w0 + c2 * (2 * MOD_PIECES) + (PC_MOD + MOD_PIECES * u),
                              s0 + c2 * (2 * GROUP * MC) + (S_MH + GROUP * MC * u),
                              c0 + c2 * (2 * GROUP * KT) + (C_MOD + GROUP * KT * u),
                              MOD_PIECES, attn_in + cms_in, cms_ready)

            def adapt(r, amid=None):
                w0, s0, c0 = r * PC_ROUND + PC_FOLD, r * S_ROUND, r * C_ROUND
                for b in range(GROUP):
                    pe.wait_ge(w_lo, w0 + (PC_ADA + 2 * b + 1))
                    for m in range(MC):
                        pe.wait_ge(hi_ready, s0 + (S_Z - GROUP * MC + MC * b + m + 1))
                        tile(bank[MC * b + m][:, :],
                             [(*slot_w(b, 0, k * HC + m * P, k * HC + (m + 1) * P), vc_hi[:, b, k, :], vc_lo[:, b, k, :])
                              for k in range(KT)],
                             (lambda k: pe.wait_ge(lo_ready, s0 + (S_Z + KT * b + k + 1))) if m == 0 else None)
                for b in range(GROUP):
                    pe.wait_ge(w_lo, w0 + (PC_ADA + 2 * b + 2))
                    pe.wait_ge(lo_ready, s0 + (S_AH + MC * (b + 1)))
                    for m in range(KT):
                        if b == 0:
                            pe.wait_ge(acc_added, c0 + (C_UP - KT + m + 1))
                        tile(bank[(4 if b == 0 else 0) + m][:, :],
                             [(*slot_w(b, 1, k * D + m * P, k * D + (m + 1) * P),
                               ph_hi[:, MC * b + k, :], ph_lo[:, MC * b + k, :]) for k in range(MC)])
                        if b == 1 and amid:
                            amid(m)

            def last_stat(what, b, tiles=range(KT)):
                r = ROUNDS - 1
                for k in tiles:
                    n = KT * b + k
                    if what == 0:
                        pe.wait_ge(acc_added, r * C_ROUND + C_UP + n + 1)
                    else:
                        pe.wait_ge(squared, r * (GROUP * KT) + n + 1)
                    done = pe.matmul(bank[4 + 2 * what + b][:, :], mean_f[:, :], (pc if what else xs[:, 1])[:, b, k, :],
                                     start=k == 0, stop=k == KT - 1)
                    if k == KT - 1:
                        done.then_inc(stat_done, 1)

            def last_amid(m):
                if m == 0:
                    last_stat(0, 0)
                else:
                    last_stat(0, 1, range(m - 1, m) if m < KT - 1 else range(m - 1, KT))
                if m == 2:
                    last_stat(1, 0)

            for f in range(FOLDS):
                fold(f)
            pe.wait_ge(const_ready, 2)
            attend(0, None)
            with pe.Fori(0, ROUNDS - 1) as r:
                mlp(r)
                adapt(r)
                attend(r + 1, r)
            mlp(ROUNDS - 1)
            adapt(ROUNDS - 1, last_amid)
            last_stat(1, 1)

        @block.scalar
        def _(act):
            def split_hi(slot, w_at, k, pieces, free_at, first=0):
                act.wait_ge(mm_done, free_at)
                for q in range(first, pieces):
                    half = (w_at + (k + q - (k + q) % 2 - PC_FOLD)) // 2
                    act.wait_ge(stage_in[(k + q) % 2], half * 16 + 16)
                    act.activation(ring[:, slot, 0, q, :], stage(k + q), ACT.Copy).then_inc(w_hi, 1)

            def plain_hi(m_at, src, dst):
                for m in range(KT):
                    act.wait_ge(mm_done, m_at + (m + 1))
                    act.activation(dst(m), src(m), ACT.Copy).then_inc(hi_ready, 1)

            def exps(r, b, banks):
                for m in range(KT):
                    at = KT * b + m
                    act.wait_ge(nmax_ready, r * (GROUP * KT) + (at + 1))
                    act.activation(pc[:, b, m, :], banks[m][:, :], ACT.Exp, bias=nmax[:, at:at + 1], scale=SCALE,
                                   accum_out=rsum[:, at:at + 1]).then_inc(exp_done, 1)

            def hidden(m_at, s_at, bias):
                for j in range(GROUP * MC):
                    act.wait_ge(mm_done, m_at + (j + 1))
                    act.wait_ge(lo_ready, s_at + (j - 1))
                    act.sem_inc(act_passed, 1)
                    act.activation(graw[:, j % 2, :], bank[j][:, :], ACT.Gelu, bias=bias(j)).then_inc(raw_ready, 1)
                    act.activation(ph_hi[:, j, :], bank[j][:, :], ACT.Gelu, bias=bias(j)).then_inc(hi_ready, 1)

            def x_split(r, b):
                for k in range(KT):
                    act.activation(xa_hi[:, b, k, :], xs_tile(r % 2, b, k), ACT.Copy).then_inc(x_hi, 1)

            def attend(r, before):
                w0, m0, s0 = r * PC_ROUND + PC_FOLD, r * M_ROUND + M_FOLD, r * S_ROUND
                layer = r // 2
                if before is not None:
                    norm_sums(before, 0)
                plain_hi(m0 + M_Y0, lambda m: bank[m][:, :], lambda m: yp_hi[:, m, :])
                x_split(r, 1)
                if before is not None:
                    norm_squares(before)
                    norm_sums(before, 1)
                plain_hi(m0 + M_V0, lambda m: bank[V0_BANKS[m]][:, :], lambda m: vc_hi[:, 0, m, :])
                exps(r, 0, bank[0:4])
                if before is not None:
                    norm_std(before, (6, 7))
                plain_hi(m0 + M_Y1, lambda m: bank[4 + m][:, :], lambda m: yp_hi[:, m, :])
                split_hi(0, w0, PC_CMS, CMS_PIECES, m0 + M_V1)
                plain_hi(m0 + M_V1, lambda m: bank[m][:, :], lambda m: vc_hi[:, 1, m, :])
                plain_hi(m0 + M_T0, lambda m: bank[4 + m][:, :], lambda m: ph_hi[:, m, :])
                exps(r, 1, bank[0:4])
                def attn_hi(b, m):
                    act.wait_ge(mm_done, m0 + ((M_O0, M_O1)[b][m] + 1))
                    act.sem_inc(act_passed, 1)
                    act.activation(xa_hi[:, b, m, :], bank[4 + m][:, :], ACT.Identity,
                                   bias=column(vec, layer, BP + m)).then_inc(hi_ready, 1)

                attn_hi(0, 0)
                attn_hi(0, 1)
                plain_hi(m0 + M_T1, lambda m: bank[m][:, :], lambda m: yp_hi[:, m, :])
                attn_hi(0, 2)
                attn_hi(0, 3)
                for m in range(KT):
                    attn_hi(1, m)

            def mlp(r):
                w0, m0, s0, c0 = r * PC_ROUND + PC_FOLD, r * M_ROUND + M_FOLD, r * S_ROUND, r * C_ROUND
                layer = r // 2

                def chunk(c2, u, per, w_first, m_first, s_first, b_first, pieces_next):
                    m_at = m0 + c2 * (2 * M_CHUNK) + (m_first + M_CHUNK * u)
                    if pieces_next:
                        split_hi(1 - u, w0 + c2 * (2 * per), w_first + per * (u + 1), pieces_next, m_at)
                    hidden(m_at, s0 + c2 * (2 * GROUP * MC) + (s_first + GROUP * MC * u),
                           lambda j: column(vec, layer, c2 * (2 * MC) + (b_first + MC * u + j % MC)))

                with act.Fori(0, CH // 2 - 1) as c2:
                    for u in range(2):
                        chunk(c2, u, CMS_PIECES, PC_CMS, M_CMS, S_CH, CB1, CMS_PIECES)
                for u in range(2):
                    chunk(CH // 2 - 1, u, CMS_PIECES, PC_CMS, M_CMS, S_CH, CB1, (CMS_PIECES, MOD_PIECES)[u])
                for n in range(GROUP * KT):
                    act.wait_ge(acc_added, c0 + (C_MOD - GROUP * KT + n + 1))
                    act.activation(vc_hi[:, n // KT, n % KT, :], pc[:, n // KT, n % KT, :], ACT.Identity,
                                   bias=column(cbias, r * 2 + n // KT, n % KT)).then_inc(hi_ready, 1)
                with act.Fori(0, CH // 2 - 1) as c2:
                    for u in range(2):
                        chunk(c2, u, MOD_PIECES, PC_MOD, M_MOD, S_MH, MB1, MOD_PIECES)
                for u in range(2):
                    chunk(CH // 2 - 1, u, MOD_PIECES, PC_MOD, M_MOD, S_MH, MB1, (MOD_PIECES, 2)[u])

            def adapt(r, more):
                w0, m0, s0 = r * PC_ROUND + PC_FOLD, r * M_ROUND + M_FOLD, r * S_ROUND
                g = r % 2
                for b in range(GROUP):
                    for k in range(KT):
                        act.wait_ge(z_ready, r * (GROUP * KT) + (KT * b + k + 1))
                        act.activation(vc_hi[:, b, k, :], xs_tile(g, b, k), ACT.Copy).then_inc(hi_ready, 1)
                    split_hi(1, w0, PC_ADA + 2, b + 1, m0 + M_DOWN, b)
                hidden(m0 + M_DOWN, s0 + S_AH, lambda j: column(avec, r * 2 + j // MC, BD + j % MC))
                if more:
                    x_split(r + 1, 0)
                    split_hi(0, w0, PC_ROUND + PC_A, 2, m0 + (M_UP + KT))
                    split_hi(1, w0, PC_ROUND + PC_U, 2, m0 + M_ROUND)

            def norm_sums(r, what):
                for b in range(GROUP):
                    act.wait_ge(sum_step, r * 12 + (6 * what + 3 * b + 3))
                    act.activation(ls_hi[:, b, :], lsum[:, b, :], ACT.Copy).then_inc(ls_hi_ready, 1)

            def norm_squares(r):
                g = r % 2
                for n in range(GROUP * KT):
                    act.wait_ge(centred, r * (GROUP * KT) + (n + 1))
                    if n % KT >= 2:
                        act.wait_ge(sum_step, r * 12 + (6 + 3 * (n // KT) + n % KT - 1))
                    elif n >= KT:
                        act.wait_ge(sum_step, r * 12 + (6 + 3))
                    act.sem_inc(act_passed, 1)
                    act.activation(graw[:, n % 2, :], xs_tile(g, n // KT, n % KT), ACT.Square).then_inc(squared, 1)

            def norm_std(r, banks, at=(3, 4), batches=range(GROUP)):
                for b in batches:
                    act.wait_ge(stat_done, r * 4 + at[b])
                    act.activation(lsum[:, b, :], bank[banks[b]][:, :], ACT.Sqrt, bias=eps[:, :]).then_inc(std_ready, 1)

            def fold_hi(f):
                if f >= 2:
                    act.wait_ge(mm_done, KT * (f - 1))
                for n, q in enumerate(FOLD_ORDER):
                    act.wait_ge(fold_in[n], 16 * (f + 1))
                    act.activation(fold_piece(f, q)[0], fold_stage(n), ACT.Copy).then_inc(w_hi, 1)

            def fold_copy(f):
                if f >= 2:
                    act.wait_ge(fold_out[f % 2], 16)
                for m in range(KT):
                    act.wait_ge(mm_done, KT * f + m + 1)
                    act.activation(pc[:, f % 2, m, :], bank[4 * (f % 2) + m][:, :], ACT.Copy).then_inc(fold_raw, 1)
                act.wait_ge(fold_raw, KT * (f + 1))
                act.dma_start(folded[f].rearrange("q p n -> p q n"),
                              pc[:, f % 2, :, :].rearrange("p (q k) n -> p q (k n)", q=2)).then_inc(fold_out[f % 2], 16)

            fold_hi(0)
            fold_hi(1)
            act.dma_start(xs[:, 0, :, :, :], x_t[0]).then_inc(x_in[0], 16)
            fold_copy(0)
            fold_hi(2)
            fold_copy(1)
            fold_hi(3)
            act.wait_ge(x_in[0], 16)
            x_split(0, 0)
            fold_copy(2)
            split_hi(0, PC_FOLD, PC_A, 2, KT)
            split_hi(1, PC_FOLD, PC_U, 2, KT)
            act.wait_ge(w_lo, PC_FOLD)
            act.dma_start(xs[:, 1, :, :, :], x_t[1]).then_inc(x_in[1], 16)
            fold_copy(3)
            act.wait_ge(fold_out[0], 16 * LAYERS)
            act.wait_ge(fold_out[1], 16 * LAYERS)
            act.wait_ge(small_in, 32)
            act.wait_ge(avec_in, 16 * LAYERS * BATCHES)
            act.wait_ge(cbias_ready, LAYERS * BATCHES)
            attend(0, None)
            act.wait_ge(x_in[1], 16)
            with act.Fori(0, ROUNDS - 1) as r:
                mlp(r)
                adapt(r, True)
                attend(r + 1, r)
            mlp(ROUNDS - 1)
            adapt(ROUNDS - 1, False)
            last = (ROUNDS - 1) * GROUP * KT
            for b in range(GROUP):
                for k in range(KT):
                    act.wait_ge(centred, last + KT * b + k + 1)
                    act.activation(pc[:, b, k, :], xs[:, 1, b, k, :], ACT.Square).then_inc(squared, 1)
                norm_std(ROUNDS - 1, (6, 7), (2, 4), (b,))
            for n in range(GROUP * KT):
                act.wait_ge(scaled, last + n + 1)
                row = 2 * (ROUNDS - 1) + n // KT
                act.activation(xs[:, 1, n // KT, n % KT, :], xs[:, 1, n // KT, n % KT, :], ACT.Identity,
                               scale=column(avec, row, GA + n % KT), bias=column(avec, row, BE + n % KT)).then_inc(x_final, 1)

        @block.vector
        def _(dve):
            def split_lo(slot, w_at, k, pieces, first=0):
                for q in range(first, pieces):
                    dve.wait_ge(w_hi, w_at + (k + q + 1))
                    dve.tensor_tensor(ring[:, slot, 1, q, :], stage(k + q), f32(ring[:, slot, 0, q, :]),
                                      ALU.subtract).then_inc(w_lo, 1)

            def plain_lo(s_at, src, hi, lo, n=KT):
                for m in range(n):
                    dve.wait_ge(hi_ready, s_at + (m + 1))
                    dve.tensor_tensor(lo(m), src(m), f32(hi(m)), ALU.subtract).then_inc(lo_ready, 1)

            def softmax(r, b, m_at, banks):
                e0 = r * (GROUP * KT)

                def normalize(m):
                    at = KT * b + m
                    dve.wait_ge(exp_done, e0 + (at + 1))
                    dve.reciprocal(rinv[:, at:at + 1], rsum[:, at:at + 1]).then_inc(rinv_done, 1)
                    dve.wait_ge(rinv_done, e0 + (at + 1))
                    dve.tensor_scalar(pc[:, b, m, :], pc[:, b, m, :], rinv[:, at:at + 1], None, ALU.mult).then_inc(p_ready, 1)

                for m in range(KT):
                    at = KT * b + m
                    dve.wait_ge(mm_done, m_at + (m + 1))
                    dve.reduce_max(smax[:, at:at + 1], banks[m][:, :], AX.X).then_inc(smax_done, 1)
                    dve.wait_ge(smax_done, e0 + (at + 1))
                    dve.tensor_scalar(nmax[:, at:at + 1], smax[:, at:at + 1], -SCALE, None, ALU.mult).then_inc(nmax_ready, 1)
                    if m:
                        normalize(m - 1)
                normalize(KT - 1)

            def zero(b):
                for m in range(KT):
                    dve.memset(pc[:, b, m, :], 0.0).then_inc(acc_added, 1)

            def attend(r, before):
                w0, m0, s0 = r * PC_ROUND + PC_FOLD, r * M_ROUND + M_FOLD, r * S_ROUND
                layer = r // 2
                if before is not None:
                    norm_sums(before)
                    split_lo(1, w0, PC_U, 2)
                plain_lo(s0 + S_Y0, lambda m: bank[m][:, :], lambda m: yp_hi[:, m, :], lambda m: yp_lo[:, m, :])
                x_split(r, 1)
                if before is not None:
                    norm_centre(before, 0)
                    norm_centre(before, 1)
                    norm_square_sums(before)
                plain_lo(s0 + S_V0, lambda m: bank[V0_BANKS[m]][:, :], lambda m: vc_hi[:, 0, m, :], lambda m: vc_lo[:, 0, m, :])
                softmax(r, 0, m0 + M_S0, bank[0:4])
                plain_lo(s0 + S_Y1, lambda m: bank[4 + m][:, :], lambda m: yp_hi[:, m, :], lambda m: yp_lo[:, m, :])
                if before is not None:
                    norm_rstd(before, 0)
                split_lo(0, w0, PC_CMS, CMS_PIECES)
                plain_lo(s0 + S_V1, lambda m: bank[m][:, :], lambda m: vc_hi[:, 1, m, :], lambda m: vc_lo[:, 1, m, :])
                if before is not None:
                    norm_scale(before, 0)
                plain_lo(s0 + S_P0, lambda m: bank[4 + m][:, :], lambda m: ph_hi[:, m, :], lambda m: ph_lo[:, m, :])
                if before is not None:
                    norm_rstd(before, 1)
                    norm_affine(before, 0)
                softmax(r, 1, m0 + M_S1, bank[0:4])
                if before is not None:
                    norm_scale(before, 1)

                def attn_lo(b, m):
                    dve.wait_ge(hi_ready, s0 + ((S_O0, S_O1)[b][m] + 1))
                    dve.scalar_tensor_tensor(xa_lo[:, b, m, :], bank[4 + m][:, :], column(vec, layer, BP + m),
                                             f32(xa_hi[:, b, m, :]), ALU.add, ALU.subtract).then_inc(lo_ready, 1)

                attn_lo(0, 0)
                attn_lo(0, 1)
                plain_lo(s0 + S_P1, lambda m: bank[m][:, :], lambda m: yp_hi[:, m, :], lambda m: yp_lo[:, m, :])
                attn_lo(0, 2)
                attn_lo(0, 3)
                zero(0)
                if before is not None:
                    norm_affine(before, 1)
                for m in range(KT):
                    attn_lo(1, m)
                zero(1)

            def mlp(r):
                w0, m0, s0, c0 = r * PC_ROUND + PC_FOLD, r * M_ROUND + M_FOLD, r * S_ROUND, r * C_ROUND
                g = r % 2

                def chunk(c2, u, per, w_first, m_first, s_first, c_first, pieces_next, acc, each=None, after=None):
                    if pieces_next:
                        split_lo(1 - u, w0 + c2 * (2 * per), w_first + per * (u + 1), pieces_next)
                    s_at = s0 + c2 * (2 * GROUP * MC) + (s_first + GROUP * MC * u)
                    plain_lo(s_at, lambda j: graw[:, j % 2, :], lambda j: ph_hi[:, j, :], lambda j: ph_lo[:, j, :], GROUP * MC)
                    m_at = m0 + c2 * (2 * M_CHUNK) + (m_first + M_CHUNK * u + GROUP * MC)
                    c_at = c0 + c2 * (2 * GROUP * KT) + (c_first + GROUP * KT * u)
                    for n in range(GROUP * KT):
                        dve.wait_ge(mm_done, m_at + (n + 1))
                        dve.wait_ge(acc_added, c_at + (n - 7))
                        dve.tensor_tensor(acc(n), acc(n), bank[4 + n % KT][:, :], ALU.add).then_inc(acc_added, 1)
                        if each:
                            dve.wait_ge(acc_added, c_at + (n + 1))
                            each(n)
                        if after and n % KT == KT - 1:
                            after(n // KT)

                def cms_acc(n):
                    return pc[:, n // KT, n % KT, :]

                def mod_acc(n):
                    return xs_tile(g, n // KT, n % KT)

                def cms_lo(b):
                    for k in range(KT):
                        dve.wait_ge(hi_ready, s0 + (S_CMS + KT * b + k + 1))
                        dve.scalar_tensor_tensor(vc_lo[:, b, k, :], pc[:, b, k, :], column(cbias, r * 2 + b, k),
                                                 f32(vc_hi[:, b, k, :]), ALU.add, ALU.subtract).then_inc(lo_ready, 1)

                def clip(n):
                    dve.tensor_scalar(mod_acc(n), mod_acc(n), 0.0, 1.0, ALU.max, ALU.min).then_inc(z_ready, 1)

                def z_lo(b):
                    if b == 1:
                        split_lo(1, w0, PC_ADA + 2, 1)
                    plain_lo(s0 + (S_Z + KT * b), lambda k: xs_tile(g, b, k), lambda k: vc_hi[:, b, k, :],
                             lambda k: vc_lo[:, b, k, :])

                with dve.Fori(0, CH // 2 - 1) as c2:
                    for u in range(2):
                        chunk(c2, u, CMS_PIECES, PC_CMS, M_CMS, S_CH, C_CMS, CMS_PIECES, cms_acc)
                for u in range(2):
                    chunk(CH // 2 - 1, u, CMS_PIECES, PC_CMS, M_CMS, S_CH, C_CMS, (CMS_PIECES, MOD_PIECES)[u], cms_acc,
                          after=cms_lo if u else None)
                for n in range(GROUP * KT):
                    b, k = n // KT, n % KT
                    dve.scalar_tensor_tensor(xs_tile(g, b, k), pc[:, b, k, :], column(xbias, r * 2 + b, k),
                                             xs_tile(g, b, k), ALU.add, ALU.add).then_inc(res_added, 1)
                dve.wait_ge(res_added, r * (GROUP * KT) + GROUP * KT)
                dve.sem_inc(dve_passed, 1)
                with dve.Fori(0, CH // 2 - 1) as c2:
                    for u in range(2):
                        chunk(c2, u, MOD_PIECES, PC_MOD, M_MOD, S_MH, C_MOD, MOD_PIECES, mod_acc)
                for u in range(2):
                    chunk(CH // 2 - 1, u, MOD_PIECES, PC_MOD, M_MOD, S_MH, C_MOD, (MOD_PIECES, 2)[u], mod_acc,
                          clip if u else None, z_lo if u else None)

            def x_split(r, b):
                for k in range(KT):
                    dve.wait_ge(x_hi, r * (GROUP * KT) + (KT * b + k + 1))
                    dve.tensor_tensor(xa_lo[:, b, k, :], xs_tile(r % 2, b, k), f32(xa_hi[:, b, k, :]),
                                      ALU.subtract).then_inc(x_lo, 1)

            def adapt(r, more):
                w0, m0, s0 = r * PC_ROUND + PC_FOLD, r * M_ROUND + M_FOLD, r * S_ROUND
                g = r % 2
                split_lo(1, w0, PC_ADA + 2, 2, 1)
                plain_lo(s0 + S_AH, lambda j: graw[:, j % 2, :], lambda j: ph_hi[:, j, :], lambda j: ph_lo[:, j, :], GROUP * MC)
                if more:
                    x_split(r + 1, 0)
                for b in range(GROUP):
                    for k in range(KT):
                        n = KT * b + k
                        dve.wait_ge(mm_done, m0 + (M_UP + n + 1))
                        dve.scalar_tensor_tensor(xs_tile(g, b, k), bank[(4 if b == 0 else 0) + k][:, :],
                                                 column(avec, r * 2 + b, BU + k), xs_tile(g, b, k),
                                                 ALU.add, ALU.add).then_inc(acc_added, 1)
                        if not more and n == KT + 1:
                            norm_centre(r, 0, 1)
                    if more and b == 0:
                        split_lo(0, w0, PC_ROUND + PC_A, 2)

            def norm_sum3(r, what, b, terms, ready):
                at = r * 12 + (6 * what + 3 * b)
                for n in range(3):
                    if ready:
                        ready(n)
                    if n:
                        dve.wait_ge(sum_step, at + n)
                    dve.tensor_tensor(lsum[:, b, :], lsum[:, b, :] if n else terms(0), terms(n + 1),
                                      ALU.add).then_inc(sum_step, 1)

            def norm_lo(r, what):
                for b in range(GROUP):
                    dve.wait_ge(ls_hi_ready, r * 4 + (2 * what + b + 1))
                    dve.tensor_tensor(ls_lo[:, b, :], lsum[:, b, :], f32(ls_hi[:, b, :]), ALU.subtract).then_inc(ls_lo_ready, 1)

            def norm_sums(r):
                g = r % 2
                dve.wait_ge(acc_added, r * C_ROUND + C_ROUND)
                for b in range(GROUP):
                    norm_sum3(r, 0, b, lambda k: xs_tile(g, b, k), None)
                norm_lo(r, 0)

            def norm_centre(r, b, at=None):
                dve.wait_ge(stat_done, r * 4 + (b + 1 if at is None else at))
                for k in range(KT):
                    dve.tensor_tensor(xs_tile(r % 2, b, k), xs_tile(r % 2, b, k), bank[4 + b][:, :],
                                      ALU.subtract).then_inc(centred, 1)

            def norm_square_sums(r):
                for b in range(GROUP):
                    norm_sum3(r, 1, b, lambda k: graw[:, k % 2, :],
                              lambda n: dve.wait_ge(squared, r * (GROUP * KT) + (KT * b + n + 2)))
                norm_lo(r, 1)

            def norm_rstd(r, b):
                dve.wait_ge(std_ready, r * GROUP + (b + 1))
                dve.reciprocal(lsum[:, b, :], lsum[:, b, :]).then_inc(rstd_ready, 1)

            def norm_scale(r, b):
                dve.wait_ge(rstd_ready, r * GROUP + (b + 1))
                for k in range(KT):
                    dve.tensor_tensor(xs_tile(r % 2, b, k), xs_tile(r % 2, b, k), lsum[:, b, :], ALU.mult).then_inc(scaled, 1)

            def norm_affine(r, b):
                for k in range(KT):
                    dve.wait_ge(scaled, r * (GROUP * KT) + (KT * b + k + 1))
                    dve.tensor_scalar(xs_tile(r % 2, b, k), xs_tile(r % 2, b, k), column(avec, r * 2 + b, GA + k),
                                      column(avec, r * 2 + b, BE + k), ALU.mult, ALU.add).then_inc(x_final, 1)

            def fold_lo(f):
                for n, q in enumerate(FOLD_ORDER):
                    dve.wait_ge(w_hi, 4 * f + n + 1)
                    hi, lo = fold_piece(f, q)
                    dve.tensor_tensor(lo, fold_stage(n), f32(hi), ALU.subtract).then_inc(w_lo, 1)

            for f in range(FOLDS):
                fold_lo(f)
            x_split(0, 0)
            split_lo(0, PC_FOLD, PC_A, 2)
            split_lo(1, PC_FOLD, PC_U, 2)

            dve.wait_ge(iota_ready, 2)
            dve.tensor_copy(mean_w[:, :], mean_f[:, :]).then_inc(const_ready, 1)
            dve.tensor_copy(feat_f[:, :], feat_i[:, :]).then_inc(code_ready, 1)
            dve.wait_ge(small_in, 32)
            dve.tensor_copy(code_f[:, :], code_i[:, :]).then_inc(code_ready, 1)
            dve.wait_ge(code_ready, 2)
            for n in range(BATCHES):
                dve.tensor_scalar(hot[:, n, :], feat_f[:, :], code_f[:, n:n + 1], None, ALU.is_equal).then_inc(hot_ready, 1)
            dve.wait_ge(hot_ready, BATCHES)
            for layer in range(LAYERS):
                for n in range(BATCHES):
                    dve.tensor_tensor(cbias[:, BATCHES * layer + n, :], hot[:, n, :], vec[:, layer, CB2:CB2 + KT],
                                      ALU.add).then_inc(cbias_ready, 1)
            dve.wait_ge(cbias_ready, LAYERS * BATCHES)
            for layer in range(LAYERS):
                for n in range(BATCHES):
                    dve.tensor_tensor(xbias[:, BATCHES * layer + n, :], cbias[:, BATCHES * layer + n, :],
                                      vec[:, layer, MB2:MB2 + KT], ALU.add).then_inc(xbias_ready, 1)

            dve.wait_ge(avec_in, 16 * LAYERS * BATCHES)
            dve.wait_ge(xbias_ready, LAYERS * BATCHES)
            attend(0, None)
            with dve.Fori(0, ROUNDS - 1) as r:
                mlp(r)
                adapt(r, True)
                attend(r + 1, r)
            mlp(ROUNDS - 1)
            adapt(ROUNDS - 1, False)
            norm_centre(ROUNDS - 1, 1, 3)
            for b in range(GROUP):
                norm_rstd(ROUNDS - 1, b)
                norm_scale(ROUNDS - 1, b)


def _tiles(w):
    n = w.shape[0] // P
    return w.reshape(n, P, w.shape[1]).transpose(1, 0, 2).reshape(P, n * w.shape[1])


def _pieces(a):
    return a.reshape(P, -1, PIECE).transpose(1, 0, 2)


def _vector(v):
    return v.reshape(-1, P).T


def kernel(**inputs):
    import concourse.bacc as bacc
    from concourse.bass_utils import run_bass_kernel_spmd

    a = {k: np.asarray(v) for k, v in inputs.items()}
    cond, ada = ("L0_cond_", "L2_cond_"), ("L1_cond_", "L3_cond_")
    down_up = [("W_down", "b_down", "W_up", "b_up", "gamma", "beta"), ("W_down", "b_down", "W_up", "b_up", "ln_w", "ln_b")]

    x_t = a["x"].reshape(2, GROUP, T, KT, P).transpose(0, 4, 1, 3, 2)
    fold_w, cms_w, mod_w, vecs = [], [], [], []
    for p in cond:
        for left, right in ((a[p + "Wq"].T, a[p + "Wk"].T), (a[p + "Wv"].T, a[p + "Wp"])):
            fold_w += [_pieces(_tiles(left)), _pieces(_tiles(right))]
        for c in range(CH):
            s = slice(c * HC, (c + 1) * HC)
            cms_w += [_pieces(_tiles(a[p + "cW1"][:, s])), _pieces(_tiles(a[p + "cW2"][s]))]
            mod_w += [_pieces(_tiles(a[p + "mW1"][:, s])), _pieces(_tiles(a[p + "mW2"][s]))]
        vecs.append(np.concatenate([_vector(a[p + n]) for n in ("bp", "cb1", "cb2", "mb1", "mb2")], 1))
    ada_w, avecs = [], []
    for p, (wd, bd, wu, bu, ga, be) in zip(ada, down_up):
        for role in range(ROLES):
            ada_w += [_pieces(_tiles(a[p + wd][role])), _pieces(_tiles(a[p + wu][role]))]
            avecs.append(np.concatenate([_vector(a[p + n][role]) for n in (bd, bu, ga, be)], 1))
    arrays = {
        "x_t": x_t,
        "codes": a["itok_B_17_1546"].reshape(1, BATCHES),
        "roles": a["itok_B_1_2"].reshape(1, BATCHES),
        "fold_w": np.concatenate(fold_w), "cms_w": np.concatenate(cms_w), "mod_w": np.concatenate(mod_w),
        "ada_w": np.concatenate(ada_w),
        "vecs": np.stack(vecs).transpose(1, 0, 2), "avecs": np.stack(avecs),
    }
    arrays = {k: np.ascontiguousarray(v) for k, v in arrays.items()}
    nc = bacc.Bacc("TRN2", target_bir_lowering=False, num_devices=1, dynamic_dma_scratch_size=1024)
    args = [nc.dram_tensor(k, v.shape, mybir.dt.from_np(v.dtype), kind="ExternalInput").ap() for k, v in arrays.items()]
    out = nc.dram_tensor("out", (2, P, GROUP, KT, T), F32, kind="ExternalOutput").ap()
    build(nc, *args, out)
    got = run_bass_kernel_spmd(nc, [arrays], core_ids=[0]).results[0]["out"]
    return got.transpose(0, 2, 4, 3, 1).reshape(BATCHES, T, D)
```
